# Optimizing a Trainium2 kernel written in Bass

```python
import numpy as np
import jax
import jax.numpy as jnp

def _softmax(x, axis=-1):
    return jax.nn.softmax(x, axis=axis)

def _gelu(x):
    return jax.nn.gelu(x, approximate=True)

def _silu(x):
    return jax.nn.silu(x)

def _sigmoid(x):
    return jax.nn.sigmoid(x)

def _layernorm(x, axis=-1, eps=1e-05):
    m = jnp.mean(x, axis=axis, keepdims=True)
    v = jnp.var(x, axis=axis, keepdims=True)
    return (x - m) / jnp.sqrt(v + eps)

def _scatter_add(tgt, idx, src, axis=0):
    return tgt.at[idx].add(src)

def _segment_sum(src, seg, n):
    return jax.ops.segment_sum(src, seg, n)
kernel_name = 'mk_gnn_ffn_d2_gnn_r8_d787f3'

def setup_inputs(seed: int=0):
    np.random.seed(seed)
    _w = jnp.asarray

    def _rec_inputs():
        import jax
        import jax.numpy as jnp
        _gk = jax.random.key(seed)
        x = -0.0003713 + 1 * jax.random.normal(jax.random.fold_in(_gk, 1), (6250, 256), jnp.float32)
        _s = jax.random.randint(jax.random.fold_in(_gk, 2), (50000,), 0, 6250, jnp.int32)
        _d = jax.random.randint(jax.random.fold_in(_gk, 3), (50000,), 0, 6250, jnp.int32)
        _loop = jnp.arange(6250, dtype=jnp.int32)
        src = jnp.concatenate([_s, _d, _loop])
        dst = jnp.concatenate([_d, _s, _loop])
        _o = jnp.argsort(dst, stable=True)
        src = src[_o]
        dst = dst[_o]
        edge_weight = -7.32377e-05 + 0.176746 * jax.random.normal(jax.random.fold_in(_gk, 12), (106250,), jnp.float32)
        return (x, src, dst, edge_weight)
    x, src, dst, edge_weight = _rec_inputs()

    def _L0_gnn_setup():
        import jax, jax.numpy as jnp
        import numpy as np
        N_NODES = 6250
        NNZ = 200000
        D_FEAT = 256
        key = jax.random.key(seed)
        k_x, k_v, k_r, k_c = jax.random.split(key, 4)
        x = jax.random.normal(k_x, (N_NODES, D_FEAT), dtype=jnp.float32)
        std = 1.0 / np.sqrt(NNZ / N_NODES)
        values = jax.random.normal(k_v, (NNZ,), dtype=jnp.float32) * std
        row = jax.random.randint(k_r, (NNZ,), 0, N_NODES, dtype=jnp.int64)
        col = jax.random.randint(k_c, (NNZ,), 0, N_NODES, dtype=jnp.int64)
        return {'x': x, 'values': values, 'row': row, 'col': col}
    _L0_gnn_all = _L0_gnn_setup()
    _L0_gnn_in = {k: v for k, v in _L0_gnn_all.items() if k in ()}
    del _L0_gnn_all

    def _L0_ffn_setup():
        import jax, jax.numpy as jnp
        import numpy as np
        TOP_K = 2
        LN_EPS = 1e-05
        key = jax.random.key(seed)
        ks = jax.random.split(key, 8)
        B, S, D, E, H = (16, 1024, 256, 8, 1024)
        x = jax.random.normal(ks[0], (B, S, D), dtype=jnp.float32)
        Wr = jax.random.normal(ks[1], (D, E), dtype=jnp.float32) * 0.1
        br = jnp.zeros((E,), dtype=jnp.float32)
        ln_g = jnp.ones((E, D), dtype=jnp.float32)
        ln_b = jnp.zeros((E, D), dtype=jnp.float32)
        W1 = jax.random.normal(ks[2], (E, D, H), dtype=jnp.float32) * (1.0 / np.sqrt(D))
        b1 = jnp.zeros((E, H), dtype=jnp.float32)
        W2 = jax.random.normal(ks[3], (E, H, D), dtype=jnp.float32) * (1.0 / np.sqrt(H))
        b2 = jnp.zeros((E, D), dtype=jnp.float32)
        return {'x': x, 'Wr': Wr, 'br': br, 'ln_g': ln_g, 'ln_b': ln_b, 'W1': W1, 'b1': b1, 'W2': W2, 'b2': b2}
    _L0_ffn_all = _L0_ffn_setup()
    _L0_ffn_in = {k: v for k, v in _L0_ffn_all.items() if k in ('Wr', 'br', 'ln_g', 'ln_b', 'W1', 'b1', 'W2', 'b2')}
    del _L0_ffn_all

    def _L1_gnn_setup():
        import jax, jax.numpy as jnp
        import numpy as np
        N = 6250
        E = 200000
        D = 256
        H = 256
        EPS = 1e-05

        def _gcn_conv(x, src, dst, W, b):
            ones = jnp.ones((src.shape[0],), x.dtype)
            deg_out = jnp.maximum(jax.ops.segment_sum(ones, src, num_segments=N), 1.0)
            deg_in = jnp.maximum(jax.ops.segment_sum(ones, dst, num_segments=N), 1.0)
            h = x * (deg_out ** (-0.5))[:, None]
            h = h @ W
            m = jax.ops.segment_sum(h[src], dst, num_segments=N)
            return m * (deg_in ** (-0.5))[:, None] + b

        def _layer_norm(h, gamma, beta):
            mu = jnp.mean(h, axis=-1, keepdims=True)
            var = jnp.mean(jnp.square(h - mu), axis=-1, keepdims=True)
            return (h - mu) * jax.lax.rsqrt(var + EPS) * gamma + beta
        key = jax.random.key(seed)
        ks = jax.random.split(key, 9)
        x = jax.random.normal(ks[0], (N, D), jnp.float32)
        src = jax.random.randint(ks[1], (E,), 0, N)
        dst = jax.random.randint(ks[2], (E,), 0, N)
        W1 = jax.random.normal(ks[3], (D, H), jnp.float32) / np.sqrt(D).astype(np.float32)
        b1 = jnp.zeros((H,), jnp.float32)
        W2 = jax.random.normal(ks[4], (H, H), jnp.float32) / np.sqrt(H).astype(np.float32)
        b2 = jnp.zeros((H,), jnp.float32)
        gamma = jnp.ones((H,), jnp.float32)
        beta = jnp.zeros((H,), jnp.float32)
        return {'x': x, 'W1': W1, 'b1': b1, 'W2': W2, 'b2': b2, 'gamma': gamma, 'beta': beta, 'src': src, 'dst': dst}
    _L1_gnn_all = _L1_gnn_setup()
    _L1_gnn_in = {k: v for k, v in _L1_gnn_all.items() if k in ('W1', 'b1', 'W2', 'b2', 'gamma', 'beta')}
    del _L1_gnn_all

    def _L1_ffn_setup():
        import jax, jax.numpy as jnp
        import numpy as np
        B, S, D = (8, 512, 256)
        H = 4 * D
        CAPACITY = 0.5
        key = jax.random.key(seed)
        ks = jax.random.split(key, 6)
        x = jax.random.normal(ks[0], (B, S, D), dtype=jnp.float32)
        attention_mask = jnp.zeros((B, 1, 1, S), dtype=jnp.float32)
        wr = jax.random.normal(ks[1], (D, 1), dtype=jnp.float32) * 0.02
        br = jnp.zeros((1,), dtype=jnp.float32)
        w1 = jax.random.normal(ks[2], (D, H), dtype=jnp.float32) * 0.02
        b1 = jnp.zeros((H,), dtype=jnp.float32)
        w2 = jax.random.normal(ks[3], (H, D), dtype=jnp.float32) * 0.02
        b2 = jnp.zeros((D,), dtype=jnp.float32)
        return {'x': x, 'attention_mask': attention_mask, 'wr': wr, 'br': br, 'w1': w1, 'b1': b1, 'w2': w2, 'b2': b2}
    _L1_ffn_all = _L1_ffn_setup()
    _L1_ffn_in = {k: v for k, v in _L1_ffn_all.items() if k in ('attention_mask', 'wr', 'br', 'w1', 'b1', 'w2', 'b2')}
    del _L1_ffn_all
    return {'x': x, 'src': src, 'dst': dst, 'edge_weight': edge_weight, 'L0_ffn_Wr': _L0_ffn_in['Wr'], 'L0_ffn_br': _L0_ffn_in['br'], 'L0_ffn_ln_g': _L0_ffn_in['ln_g'], 'L0_ffn_ln_b': _L0_ffn_in['ln_b'], 'L0_ffn_W1': _L0_ffn_in['W1'], 'L0_ffn_b1': _L0_ffn_in['b1'], 'L0_ffn_W2': _L0_ffn_in['W2'], 'L0_ffn_b2': _L0_ffn_in['b2'], 'L1_gnn_W1': _L1_gnn_in['W1'], 'L1_gnn_b1': _L1_gnn_in['b1'], 'L1_gnn_W2': _L1_gnn_in['W2'], 'L1_gnn_b2': _L1_gnn_in['b2'], 'L1_gnn_gamma': _L1_gnn_in['gamma'], 'L1_gnn_beta': _L1_gnn_in['beta'], 'L1_ffn_attention_mask': _L1_ffn_in['attention_mask'], 'L1_ffn_wr': _L1_ffn_in['wr'], 'L1_ffn_br': _L1_ffn_in['br'], 'L1_ffn_w1': _L1_ffn_in['w1'], 'L1_ffn_b1': _L1_ffn_in['b1'], 'L1_ffn_w2': _L1_ffn_in['w2'], 'L1_ffn_b2': _L1_ffn_in['b2']}

def reference(x, src, dst, edge_weight, L0_ffn_Wr, L0_ffn_br, L0_ffn_ln_g, L0_ffn_ln_b, L0_ffn_W1, L0_ffn_b1, L0_ffn_W2, L0_ffn_b2, L1_gnn_W1, L1_gnn_b1, L1_gnn_W2, L1_gnn_b2, L1_gnn_gamma, L1_gnn_beta, L1_ffn_attention_mask, L1_ffn_wr, L1_ffn_br, L1_ffn_w1, L1_ffn_b1, L1_ffn_w2, L1_ffn_b2):
    import jax
    import jax.numpy as jnp

    def _L0_gnn_ref(x, values, row, col):
        import jax, jax.numpy as jnp
        import numpy as np
        N_NODES = 6250
        NNZ = 200000
        D_FEAT = 256
        msgs = values[:, None] * x[col]
        out = jax.ops.segment_sum(msgs, row, num_segments=N_NODES)
        return out

    def _L0_ffn_ref(x, Wr, br, ln_g, ln_b, W1, b1, W2, b2):
        import jax, jax.numpy as jnp
        import numpy as np
        TOP_K = 2
        LN_EPS = 1e-05
        B, S, D = x.shape
        N = B * S
        xt = x.reshape(N, D)
        logits = xt @ Wr + br
        probs = jax.nn.softmax(logits, axis=-1)
        top_p, top_idx = jax.lax.top_k(probs, TOP_K)
        weights = top_p / top_p.sum(axis=-1, keepdims=True)
        mu = xt.mean(axis=-1, keepdims=True)
        var = ((xt - mu) ** 2).mean(axis=-1, keepdims=True)
        xn = (xt - mu) * jax.lax.rsqrt(var + LN_EPS)
        xe = xn[None, :, :] * ln_g[:, None, :] + ln_b[:, None, :]
        h = jax.nn.gelu(jnp.einsum('end,edh->enh', xe, W1) + b1[:, None, :], approximate=False)
        y = jnp.einsum('enh,ehd->end', h, W2) + b2[:, None, :]
        y_tok = jnp.transpose(y, (1, 0, 2))
        sel = jnp.take_along_axis(y_tok, top_idx[:, :, None], axis=1)
        out = (weights[:, :, None] * sel).sum(axis=1)
        return out.reshape(B, S, D)

    def _L1_gnn_ref(x, W1, b1, W2, b2, gamma, beta, src, dst):
        import jax, jax.numpy as jnp
        import numpy as np
        N = 6250
        E = 200000
        D = 256
        H = 256
        EPS = 1e-05

        def _gcn_conv(x, src, dst, W, b):
            ones = jnp.ones((src.shape[0],), x.dtype)
            deg_out = jnp.maximum(jax.ops.segment_sum(ones, src, num_segments=N), 1.0)
            deg_in = jnp.maximum(jax.ops.segment_sum(ones, dst, num_segments=N), 1.0)
            h = x * (deg_out ** (-0.5))[:, None]
            h = h @ W
            m = jax.ops.segment_sum(h[src], dst, num_segments=N)
            return m * (deg_in ** (-0.5))[:, None] + b

        def _layer_norm(h, gamma, beta):
            mu = jnp.mean(h, axis=-1, keepdims=True)
            var = jnp.mean(jnp.square(h - mu), axis=-1, keepdims=True)
            return (h - mu) * jax.lax.rsqrt(var + EPS) * gamma + beta
        h = _gcn_conv(x, src, dst, W1, b1)
        h = jax.nn.relu(h)
        h = _gcn_conv(h, src, dst, W2, b2)
        h = _layer_norm(h, gamma, beta)
        return h

    def _L1_ffn_ref(x, attention_mask, wr, br, w1, b1, w2, b2):
        import jax, jax.numpy as jnp
        import numpy as np
        B, S, D = (8, 512, 256)
        H = 4 * D
        CAPACITY = 0.5
        b, s, d = x.shape
        weights = (jnp.einsum('bsd,do->bso', x, wr) + br)[..., 0]
        k = max(1, int(CAPACITY * s))
        kk = k - 1 if k > 1 else 1
        _, idx = jax.lax.top_k(weights, k)
        sel_idx = idx[:, :kk]
        sel = jnp.take_along_axis(x, sel_idx[:, :, None], axis=1)
        h = jax.nn.gelu(jnp.einsum('bkd,dh->bkh', sel, w1) + b1)
        y = jnp.einsum('bkh,hd->bkd', h, w2) + b2
        w_sel = jnp.take_along_axis(weights, sel_idx, axis=1)
        y = y * w_sel[..., None]
        batch_idx = jnp.arange(b)[:, None]
        processed = jnp.zeros_like(x).at[batch_idx, sel_idx].set(y)
        return processed + x
    x = x + _L0_gnn_ref(_layernorm(x, axis=-1), edge_weight, src, dst)
    x = x + _L0_ffn_ref(_layernorm(x, axis=-1)[None], L0_ffn_Wr, L0_ffn_br, L0_ffn_ln_g, L0_ffn_ln_b, L0_ffn_W1, L0_ffn_b1, L0_ffn_W2, L0_ffn_b2)[0]
    x = x + _L1_gnn_ref(_layernorm(x, axis=-1), L1_gnn_W1, L1_gnn_b1, L1_gnn_W2, L1_gnn_b2, L1_gnn_gamma, L1_gnn_beta, src, dst)
    x = x + _L1_ffn_ref(_layernorm(x, axis=-1)[None], L1_ffn_attention_mask, L1_ffn_wr, L1_ffn_br, L1_ffn_w1, L1_ffn_b1, L1_ffn_w2, L1_ffn_b2)[0]
    return x

_drawn_inputs = setup_inputs


def setup_inputs(seed=0):
    import zlib

    import numpy as np

    out = dict(_drawn_inputs(seed))
    spreads = {'L0_ffn_br': (0.0, 0.1),
     'L0_ffn_ln_g': (1.0, 0.2),
     'L0_ffn_ln_b': (0.0, 0.1),
     'L0_ffn_b1': (0.0, 0.1),
     'L0_ffn_b2': (0.0, 0.1),
     'L1_gnn_b1': (0.0, 0.1),
     'L1_gnn_b2': (0.0, 0.1),
     'L1_gnn_gamma': (1.0, 0.2),
     'L1_gnn_beta': (0.0, 0.1),
     'L1_ffn_b1': (0.0, 0.8),
     'L1_ffn_b2': (0.0, 0.8)}
    factors = {'L1_ffn_wr': 4.29, 'L1_ffn_w1': 8.0, 'L1_ffn_w2': 8.0}
    for name, (base, spread) in spreads.items():
        noise = np.random.default_rng([zlib.crc32(name.encode()), seed]).standard_normal(out[name].shape)
        drawn = base * np.exp(spread * noise) if base else spread * noise
        out[name] = jnp.asarray(drawn.astype(out[name].dtype))
    for name, factor in factors.items():
        out[name] = (out[name] * factor).astype(out[name].dtype)
    return out
```

```python
from contextlib import ExitStack

import concourse.bass as bass
from concourse import mybir

P = 128
ALU = mybir.AluOpType
ACT = mybir.ActivationFunctionType
F32 = mybir.dt.float32
BF16 = mybir.dt.bfloat16
I32 = mybir.dt.int32
I16 = mybir.dt.int16
AX = mybir.AxisListType
FAR = 1.0e6
EPS = 1.0e-5
IN_RANGE = "computed on the chip from counts, within its range for any input"


class Chain:

    def __init__(self, engine, sem):
        self.engine, self.sem, self.n, self.loop, self.k = engine, sem, 0, None, 0

    def __call__(self, instruction):
        instruction.then_inc(self.sem, 1)
        if self.loop is None:
            self.n += 1
            self.engine.wait_ge(self.sem, self.n)
        else:
            self.k += 1
            it, first, per = self.loop
            self.engine.wait_ge(self.sem, (it - first) * per + (self.n + self.k))

    def enter(self, it, first, per):
        self.loop, self.k = (it, first, per), 0

    def leave(self, rounds):
        _, _, per = self.loop
        assert self.k == per, (self.k, per)
        self.n += rounds * per
        self.loop = None


def gnn_program(nc, x, src, dst, edge_weight, Wr, br, ln_g, ln_b, W1, b1, W2, b2,
                gW1, gb1, gW2, gb2, gamma, beta, fwr, fbr, fw1, fb1, fw2, fb2, out):
    N, D = x.shape
    E = src.shape[0]
    NE, H = W1.shape[0], W1.shape[2]
    T = -(-N // P)
    LAST = N - (T - 1) * P
    KC = D // P
    HC = H // P
    NBLK = -(-E // P)
    TAIL = E - (NBLK - 1) * P
    U = 16
    NI = -(-(NBLK + T - 1) // U) * U
    ROUNDS = NI // U
    assert U == 16
    NIT = -(-NI // P)
    NIP = NIT * P
    W = D + 2
    EP = 125
    EC = E // EP
    assert EP * EC == E and EP < P
    CH = 7
    NCH = T // CH
    assert CH * NCH == T
    NT = (2 * N - NE) // P + NE
    NT += NT % 2
    KSEL = max(1, N // 2) - 1
    NF = -(-KSEL // P)
    FLAST = KSEL - (NF - 1) * P
    FPAD = T * P + P

    with ExitStack() as ctx:
        def sb(name, shape, dt=F32):
            return ctx.enter_context(nc.sbuf_tensor(name, shape, dt))

        def sem(name):
            return ctx.enter_context(nc.semaphore(name))

        def dram(name, shape, dt=F32):
            return nc.dram_tensor(name, shape, dt).ap()

        rec = dram("edge_blocks", [NBLK, 3, P], I32)
        msgs = dram("messages", [NBLK * P, W])
        xn2_t = dram("expert_in_rows", [T * P, D])
        x2_t = dram("residual_rows", [FPAD, D])
        conv1_t = dram("conv1_rows", [T * P, D])
        conv2_t = dram("conv2_rows", [T * P, D])
        xn4_t = dram("ffn_in_rows", [T * P, D])

        WORK = 4900
        SMALL = 2200
        reg_a = sb("reg_a", [P, NE * KC * H])
        reg_b = sb("reg_b", [P, NE * HC * D])
        tables = sb("tables", [P, 6 * NIP])
        work = sb("work", [P, WORK])
        small = sb("small", [P, SMALL])
        IOTA = sb("iota", [P, P])
        IDENT = sb("ident", [P, P])
        ONES = sb("ones", [P, P])
        TRI = sb("tri", [P, P])
        TRIB = sb("trib", [P, 2, P], BF16)
        PT = sb("param_t", [P, P])
        WRS = sb("wrs", [P, KC, NE])
        B2B = sb("b2_rows", [P, NE * D])
        BRB = sb("brb", [P, NE + 1])
        rows = sb("rows", [1, 3, NIP], I16)
        etab = sb("etab", [1, NT + 4], I32)
        slot_t = sb("slot_t", [P, 3 * (NT + 2)])

        X = reg_a[:, 0:T * D].rearrange("p (t d) -> p t d", d=D)
        w1s = reg_a[:, :].rearrange("p (e c h) -> p e c h", e=NE, c=KC)
        XNf = reg_b[:, 0:T * D]
        XN = XNf.rearrange("p (t d) -> p t d", d=D)
        ACCf = reg_b[:, 0:T * (D + 1)]
        ACC = ACCf.rearrange("p (t d) -> p t d", d=D + 1)
        w2s = reg_b[:, :].rearrange("p (e c d) -> p e c d", e=NE, c=HC)
        w1f, w2ff = reg_a[:, :], reg_b[:, :]
        recs = reg_b[:, T * D:T * D + NIT * 3 * P].bitcast(I32).rearrange("p (k a j) -> p k a j", k=NIT, a=3)
        ta = reg_a[:, T * D:]
        DG = ta[:, 0:NIP].rearrange("p (k n) -> p k n", n=P)
        RF = ta[:, NIP:NIP + NIT * 2 * P].rearrange("p (k a j) -> p k a j", k=NIT, a=2)
        CD = ta[:, NIP + NIT * 2 * P:2 * NIP + NIT * 2 * P]

        DREL = tables[:, 0:NIP]
        WT = tables[:, NIP:2 * NIP]
        SRCI = tables[:, 2 * NIP:3 * NIP].bitcast(I32)
        SB = tables[:, 3 * NIP:4 * NIP]
        OUT_OF = tables[:, 4 * NIP:5 * NIP]
        CS = tables[:, 5 * NIP:6 * NIP]
        fw1s = tables[:, 0:KC * H].rearrange("p (c h) -> p c h", c=KC)
        fw2s = tables[:, KC * H:KC * H + HC * D].rearrange("p (c d) -> p c d", c=HC)
        ROW_D, ROW_SA, ROW_SB = range(3)

        def carve(start, *sizes):
            views, at = [], start
            for n in sizes:
                views.append(work[:, at:at + n])
                at += n
            assert at <= WORK
            return views
        DSTR, SRCR, DSTF, SRCF, CMPD, CMPS, PADM, PADR = carve(0, EC + 2, EC, EC + 2, EC, EC // 2, EC // 2, W, 3 * P)
        DSTR, SRCR, PADR = DSTR.bitcast(I32), SRCR.bitcast(I32), PADR.bitcast(I32)
        CMPD, CMPS = CMPD.bitcast(BF16), CMPS.bitcast(BF16)
        G, OH, OHT = carve(0, U * W, 4 * P, 2 * P)
        G = G.rearrange("p (u w) -> p u w", w=W)
        OH = OH.rearrange("p (s n) -> p s n", s=4)
        OHT = OHT.rearrange("p (s n) -> p s n", s=2)
        XR, XT, ZB = carve(0, 2 * CH * D, 2 * D, 2 * D)
        XR = XR.rearrange("p (s t d) -> p s t d", s=2, d=D)
        XT = XT.rearrange("p (s c n) -> p s c n", s=2, c=KC)
        ZB = ZB.rearrange("p (s d) -> p s d", s=2)
        TE = T * NE
        LG, PR, EQ, OHB, TOT, INC, TI, A_OH, B_OH = carve(
            0, TE, TE, TE, 2 * TE, 2 * TE, 2 * TE, 4 * T, 2 * P, 2 * 2 * NT)
        A_OH = A_OH.rearrange("p (s n) -> p s n", s=2)
        B_OH = B_OH.rearrange("p (s n) -> p s n", s=2)
        IDT = INC[:, TE:TE + T]
        GT = INC[:, TE + T:TE + 3 * T].rearrange("p (s t) -> p s t", s=2)
        PR3, EQ3, LG3 = (a_.rearrange("p (t e) -> p t e", e=NE) for a_ in (PR, EQ, LG))
        OH1, OH2 = (OHB[:, k * TE:(k + 1) * TE].rearrange("p (t e) -> p t e", e=NE) for k in range(2))
        EXC, PA = TOT[:, 0:TE], TOT[:, TE:2 * TE].rearrange("p (t e) -> p t e", e=NE)
        HILO = TI[:, 0:4 * T].rearrange("p (h s t) -> p h s t", h=2, s=2)
        TII = EQ[:, 0:4 * T].bitcast(I32).rearrange("p (h s t) -> p h s t", h=2, s=2)
        HS, HTS, GX, XE, YT, YO, NIDX = carve(0, H, H, 2 * D, 2 * D, D, 2 * D, 4)
        HTS = HTS.rearrange("p (c n) -> p c n", c=HC)
        GX = GX.rearrange("p (s d) -> p s d", s=2)
        XE = XE.rearrange("p (s c n) -> p s c n", s=2, c=KC)
        YO = YO.rearrange("p (s d) -> p s d", s=2)
        GIDX, SIDX = NIDX[:, 0:2].bitcast(I32), NIDX[:, 2:4].bitcast(I32)

        tb = reg_b[:, T * (D + 1):]
        gws = tb[:, 0:2 * KC * D].rearrange("p (l c d) -> p l c d", l=2, c=KC)
        GB1B, GB2B, GAMB, BETB, FB2B, FWRB = (tb[:, 2 * KC * D + k * D:2 * KC * D + (k + 1) * D] for k in range(6))
        FBR = BRB[:, NE:NE + 1]
        gate_t, gidx_t, sidx_t = (slot_t[:, k * (NT + 2):(k + 1) * (NT + 2)] for k in range(3))
        gidx_t, sidx_t = gidx_t.bitcast(I32), sidx_t.bitcast(I32)
        taken = [0]

        def sm(n):
            taken[0] += n
            return small[:, taken[0] - n:taken[0]]
        BOH = sm(4 * 26).bitcast(BF16).rearrange("p (s n) -> p s n", s=4)
        STG, PIDX = sm(U).bitcast(I32), sm(U).bitcast(I32)
        POS, JUNK = sm(4), sm(64)
        CNT = sm(104)
        ZERO = sm(2 * NT)
        MV = sm(4 * T).rearrange("p (s t k) -> p s t k", s=2, k=2)
        MV6 = sm(2 * 6 * CH).rearrange("p (s t k) -> p s t k", s=2, k=6)
        SQ, RS, NB = (sm(2 * T).rearrange("p (s t) -> p s t", s=2) for _ in range(3))
        DO, DI, T1 = sm(T), sm(T), sm(T)
        EPSC, ZEROC, PCOL = sm(1), sm(1), sm(1)
        SGN = sm(T - 1)
        J7 = sm(NIT)
        ST, STI, BLF, ENF, NB49, INCL, OFF, KK, DK, TJ = (sm(T + 1) for _ in range(10))
        STS = sm(T + 1)
        BSEL, KSL, ATB, ATK, ATC = (sm(NIT) for _ in range(5))
        BLKI = sm(NIT).bitcast(I32)
        STI = STI.bitcast(I32)
        VAL = sm(T)
        WV = sm(T)
        RM, PK = sm(T), sm(2 * T).rearrange("p (s t) -> p s t", s=2)
        DESC, TOFF, TLN, PB = (sm(NE) for _ in range(4))
        TLI = sm(NE).bitcast(I32)
        SC = sm(16)
        assert taken[0] <= SMALL, taken[0]

        ps = [ctx.enter_context(nc.psum_tensor(f"bank{k}", [P, 512], F32)) for k in range(8)]
        sems = {}

        def z(name):
            if name not in sems:
                sems[name] = ctx.enter_context(nc.semaphore(name))
            return sems[name]

        def nodes(a, c, n=CH):
            return a[c * CH * P:(c * CH + n) * P, :].rearrange("(t p) d -> p t d", p=P)

        def row1(a, n):
            return a.rearrange("(a n) -> a n", a=1).to_broadcast([P, n])

        def load4(engine, row, i, most):
            return nc.values_load_multi_w_load_instructions(
                rows[0:1, row, bass.ds(i, 4)], engines=[engine], min_val=0, max_val=most,
                skip_runtime_bounds_check_because=IN_RANGE)[1]

        PE_, DVE_, SP_, ACT_ = (mybir.EngineType.PE, mybir.EngineType.DVE, mybir.EngineType.SP,
                                mybir.EngineType.Activation)
        block = ctx.enter_context(nc.Block())

        NORMS = dict(ln0=("a", 0), ln1=("a", 1), ln3=("a", 2), ln5=("a", 3), ln2=("b", 0), ln4=("b", 1))

        def norms(tag, what, c=0):
            which, before = NORMS[tag]
            return z(f"norm_{what}_{which}"), c + before * NCH

        CONST = 7
        ACC_CUT = 20 * (D + 1)
        PAR_IN = 8 * 16
        NFT = NF + NF % 2
        assert NFT * P <= N
        MOE = dict(tag="moe", tiles=NT, tiles_before=0, bias=4 * NE, gelu=ACT.Gelu, table=xn2_t, target=x2_t)
        FFN = dict(tag="ffn", tiles=NFT, tiles_before=NT, bias=4 * NE + NE * HC, gelu=ACT.Gelu_apprx_tanh, table=xn4_t, target=out)

        BEFORE = dict(p1=NI, p2=2 * NI)

        def expert(engine, j):
            return nc.values_load_multi_w_load_instructions(
                etab[0:1, bass.ds(j, 1)], engines=[engine], min_val=0, max_val=NE - 1,
                skip_runtime_bounds_check_because=IN_RANGE)[1][0]

        def per_node(a_, n=NE):
            return a_.rearrange("p (t o) -> p t o", o=1).to_broadcast([P, a_.shape[1], n])

        def per_column(a_, n):
            return a_.rearrange("p (o d) -> p o d", o=1).to_broadcast([P, n, a_.shape[1]])

        def message_loads(eng, which, half):
            for u in range(U):
                eng.wait_ge(z(f"ring_dma{u}"), 16 * ROUNDS)
            eng.wait_ge(z("msg_pad"), 16)

            def body(i0, first):
                for q in range(U // 4):
                    v = load4(which, ROW_SB, i0 + 4 * q, NBLK - 1)
                    for k in (half, half + 2):
                        u = 4 * q + k
                        if not first:
                            eng.wait_ge(z("s_mm"), i0 + u + 1 - U)
                        eng.dma_start(G[:, u, :], msgs[bass.ds(v[k] * P, P), :]).then_inc(z(f"sorted_in{u}"), 16)
            eng.wait_ge(z("rows_set"), 5)
            body(0, True)
            with eng.Fori(U, NI, U) as i0:
                body(i0, False)

        @block.sync
        def _(sp):
            sp.dma_start(DSTR[0:EP, 0:EC], dst.rearrange("(p j) -> p j", p=EP)).then_inc(z("edges_in"), 16)
            sp.dma_start(SRCR[0:EP, 0:EC], src.rearrange("(p j) -> p j", p=EP)).then_inc(z("edges_in"), 16)
            sp.wait_ge(z("pads_set"), 1)
            sp.dma_start(DSTR[0:EP - 1, EC:EC + 1],
                         dst[EC:E].rearrange("(p j) -> p j", p=EP - 1)[:, 0:1],
                         allow_slow_non_contiguous=True).then_inc(z("edges_in"), 16)
            for c in range(NCH):
                n = CH - (c == NCH - 1)
                sp.dma_start(X[:, c * CH:c * CH + n, :], nodes(x, c, n)).then_inc(z(f"x_in{c}"), 16)
            sp.dma_start(X[0:LAST, T - 1, :], x[(T - 1) * P:N, :]).then_inc(z(f"x_in{NCH - 1}"), 16)
            full = (NBLK - 1) * P
            for a, arr in enumerate((dst, src, edge_weight.bitcast(I32))):
                sp.dma_start(rec[0:NBLK - 1, a, :], arr[0:full].rearrange("(b j) -> b j", j=P)).then_inc(z("rec_in"), 16)
                sp.dma_start(rec[NBLK - 1:NBLK, a, 0:TAIL],
                             arr[full:E].rearrange("(b j) -> b j", b=1)).then_inc(z("rec_in"), 16)
                sp.dma_start(rec[NBLK - 1:NBLK, a, TAIL:P],
                             PADR[0:1, a * P:a * P + P - TAIL]).then_inc(z("rec_in"), 16)
            sp.dma_start(msgs[E:NBLK * P, :], PADM[0:NBLK * P - E, :]).then_inc(z("msg_pad"), 16)
            r = 0
            for a in (ln_g.rearrange("e (c p) -> (e c) p", p=P), ln_b.rearrange("e (c p) -> (e c) p", p=P),
                      b1.rearrange("e (c p) -> (e c) p", p=P), fb1.rearrange("(c p) -> c p", p=P)):
                sp.dma_start(PT[r:r + a.shape[0], :], a).then_inc(z("par_in"), 16)
                r += a.shape[0]
            sp.dma_start(WRS[:, :, :], Wr.rearrange("(c p) e -> p c e", p=P)).then_inc(z("par_in"), 16)
            sp.dma_start(B2B[:], row1(b2.rearrange("e d -> (e d)"), NE * D)).then_inc(z("par_in"), 16)
            sp.dma_start(BRB[:, 0:NE], row1(br, NE)).then_inc(z("par_in"), 16)
            sp.dma_start(FBR, row1(fbr, 1)).then_inc(z("par_in"), 16)

            message_loads(sp, SP_, 0)


            for c in range(NCH + 3):
                if c < NCH:
                    sp.wait_ge(z("x1_set"), c + 1)
                    sp.dma_start(nodes(x2_t, c), X[:, c * CH:(c + 1) * CH, :]).then_inc(z("x1_out"), 16)
                if c >= 3:
                    sp.wait_ge(*norms("ln2", "norm", c - 2))
                    sp.dma_start(nodes(xn2_t, c - 3), XR[:, (c - 3) % 2, :, :]).then_inc(z(f"xn2_out{(c - 3) % 2}"), 16)
            sp.dma_start(x2_t[T * P:FPAD, :], X[:, 0, :]).then_inc(z("x1_out"), 16)
            sp.wait_ge(z("x1_out"), 16 * (NCH + 1))
            sp.wait_ge(*norms("ln1", "norm", NCH))
            for e in range(NE):
                sp.dma_start(w1s[:, e, :, :], W1[e].rearrange("(c p) h -> p c h", p=P)).then_inc(z("w1_in"), 16)
            sp.wait_ge(z("rt_mm"), T)
            sp.wait_ge(*norms("ln2", "norm", NCH))
            for e in range(NE):
                sp.dma_start(w2s[:, e, :, :], W2[e].rearrange("(c p) d -> p c d", p=P)).then_inc(z("w2_in"), 16)
            for k in range(2):
                sp.wait_ge(z(f"net_added{k}"), 16 * (NT // 2))
            for c in range(NCH):
                sp.dma_start(X[:, c * CH:(c + 1) * CH, :], nodes(x2_t, c)).then_inc(z(f"x_in{c}"), 16)
            for l, a in enumerate((gW1, gW2)):
                sp.dma_start(gws[:, l, :, :], a.rearrange("(c p) d -> p c d", p=P)).then_inc(z("tail_in"), 16)
            for to, a in ((GB1B, gb1), (GB2B, gb2), (GAMB, gamma), (BETB, beta), (FB2B, fb2)):
                sp.dma_start(to, row1(a, D)).then_inc(z("tail_in"), 16)
            sp.dma_start(FWRB, row1(fwr.rearrange("d o -> (d o)"), D)).then_inc(z("tail_in"), 16)
            for c in range(NCH):
                sp.wait_ge(*norms("ln3", "norm", c + 1))
                sp.dma_start(nodes(conv1_t, c), XR[:, c % 2, :, :]).then_inc(z(f"conv1_out{c % 2}"), 16)
            for c in range(NCH):
                sp.wait_ge(z("relu1"), (c + 1) * CH)
                sp.dma_start(nodes(conv2_t, c), XR[:, c % 2, :, :]).then_inc(z(f"conv2_out{c % 2}"), 16)
            sp.wait_ge(z("p2_add"), NI + 1)
            sp.wait_ge(z("p2_stg"), NI)
            sp.dma_start(fw1s[:, :, :], fw1.rearrange("(c p) h -> p c h", p=P)).then_inc(z("fw_in"), 16)
            sp.dma_start(fw2s[:, :, :], fw2.rearrange("(c p) d -> p c d", p=P)).then_inc(z("fw_in"), 16)
            for c in range(NCH):
                n = CH - (c == NCH - 1)
                sp.wait_ge(*norms("ln4", "norm", c + 1))
                sp.dma_start(nodes(xn4_t, c), ACC[:, c * CH:(c + 1) * CH, 0:D]).then_inc(z("xn4_out"), 16)
                sp.wait_ge(z("sum_set"), c + 1)
                sp.dma_start(nodes(out, c, n), X[:, c * CH:c * CH + n, :]).then_inc(z("sum_out"), 16)
            sp.dma_start(out[(T - 1) * P:N, :], X[0:LAST, T - 1, :]).then_inc(z("sum_out"), 16)
            sp.wait_ge(z("xn4_out"), 16 * NCH)
            sp.wait_ge(z("sum_out"), 16 * (NCH + 1))
            sp.wait_ge(z("par_in"), PAR_IN)
            for k in range(2):
                sp.wait_ge(z(f"net_added{k}"), 16 * ((NT + NFT) // 2))

        @block.gpsimd
        def _(pool):
            g = nc.gpsimd
            ok = dict(allow_small_or_imprecise_dtypes=True)
            g.iota(IOTA[:], [[1, P]], base=0, channel_multiplier=0, **ok).then_inc(z("const"), 1)
            g.iota(J7, [[P, NIT]], base=0, channel_multiplier=1, **ok).then_inc(z("const"), 1)
            g.iota(PCOL, [[0, 1]], base=0, channel_multiplier=1, **ok).then_inc(z("const"), 1)
            g.memset(ONES[:], 1.0).then_inc(z("const"), 1)
            g.memset(IDENT[:], 0.0).then_inc(z("const"), 1)
            pool.wait_ge(z("const"), 5)
            g.affine_select(out=IDENT[:], in_=IDENT[:], compare_op=ALU.not_equal, fill=1.0, base=0,
                            pattern=[[1, P]], channel_multiplier=-1).then_inc(z("const"), 1)
            g.affine_select(out=TRI[:], in_=ONES[:], compare_op=ALU.is_gt, fill=0.0, base=0,
                            pattern=[[1, P]], channel_multiplier=-1).then_inc(z("const"), 1)
            pool.wait_ge(z("rec_in"), 9 * 16)
            pool.wait_ge(z("blocks_set"), 1)
            for k in range(NIT):
                g.indirect_dma_start(recs[:, k, :, :].rearrange("p a j -> p (a j)"), None,
                                     rec.rearrange("b a j -> b (a j)"),
                                     bass.IndirectOffsetOnAxis(ap=BLKI[:, k:k + 1], axis=0)
                                     ).then_inc(z("rec_out"), 16)

            pool.wait_ge(z("msg_pad"), 16)
            with pool.Fori(0, NI, U) as i0:
                for u in range(U):
                    pool.wait_ge(z("m_row"), i0 + u + 1)
                    pool.wait_ge(z("m_idx"), i0 + u + 1)
                    pool.sem_inc(z("turn"), 1)
                    pool.wait_ge(z("const"), CONST)
                    g.indirect_dma_start(msgs, bass.IndirectOffsetOnAxis(ap=PIDX[:, u:u + 1], axis=0),
                                         G[:, u, :], None, bounds_check=E - 1, oob_is_err=False
                                         ).then_inc(z(f"ring_dma{u}"), 16)
            pool.wait_ge(z("m_mm"), NI)
            g.memset(ACCf[:, ACC_CUT:], 0.0).then_inc(z("acc_zero"), 1)


            def network(tag, tiles, tiles_before, table, target, **_):
                def gather(j, s, dynamic=True):
                    pool.wait_ge(z("net_gidx"), j + 1 + tiles_before)
                    if dynamic:
                        pool.wait_ge(z("net_tr"), j - 1 + tiles_before)
                        pool.sem_inc(z("turn"), 1)
                    pool.wait_ge(z("const"), CONST)
                    g.indirect_dma_start(GX[:, s, :], None, table,
                                         bass.IndirectOffsetOnAxis(ap=GIDX[:, s:s + 1], axis=0)
                                         ).then_inc(z(f"net_in{s}"), 16)

                def scatter(j, s, first, h0):
                    pool.wait_ge(z("net_out"), j + 1 + tiles_before)
                    if not first:
                        pool.wait_ge(z(f"net_added{1 - s}"), h0 + 16 * s + tiles_before * 8)
                    pool.sem_inc(z("turn"), 1)
                    pool.wait_ge(z("const"), CONST)
                    g.indirect_dma_start(target, bass.IndirectOffsetOnAxis(ap=SIDX[:, s:s + 1], axis=0),
                                         YO[:, s, :], None, compute_op=ALU.add).then_inc(z(f"net_added{s}"), 16)
                gather(0, 0, False)
                gather(1, 1, False)
                gather(2, 0)
                scatter(0, 0, True, 0)
                gather(3, 1)
                scatter(1, 1, False, 0)
                with pool.Fori(2, tiles - 2, 2) as j0:
                    h0 = j0 * 8
                    gather(j0 + 2, 0)
                    scatter(j0, 0, False, h0)
                    gather(j0 + 3, 1)
                    scatter(j0 + 1, 1, False, h0)
                scatter(tiles - 2, 0, False, (tiles - 2) * 8)
                scatter(tiles - 1, 1, False, (tiles - 2) * 8)

            def gathers(tag, table):
                def body(i0, first):
                    for u in range(U):
                        if u % 8 == 0:
                            pool.wait_ge(z(f"{tag}_stg"), i0 + u + 8)
                        if not first:
                            pool.wait_ge(z(f"{tag}_mm"), i0 + u + 1 - U)
                        if u % 8 == 0 or not first:
                            pool.sem_inc(z("turn"), 1)
                        pool.wait_ge(z("const"), CONST)
                        g.indirect_dma_start(G[:, u, 0:D], None, table,
                                             bass.IndirectOffsetOnAxis(ap=STG[:, u:u + 1], axis=0)
                                             ).then_inc(z(f"ring_dma{u}"), 16)
                body(0, True)
                with pool.Fori(U, NI, U) as i0:
                    body(i0, False)

            pool.wait_ge(z("x1_out"), 16 * (NCH + 1))
            pool.wait_ge(z("xn2_out0"), 64)
            pool.wait_ge(z("xn2_out1"), 48)
            network(**MOE)
            for k in range(2):
                pool.wait_ge(z(f"net_added{k}"), 16 * (NT // 2))
            pool.wait_ge(z("net_mm2"), NT)
            g.memset(ACCf, 0.0).then_inc(z("acc1_zero"), 1)
            pool.wait_ge(z("conv1_out0"), 64)
            pool.wait_ge(z("conv1_out1"), 48)
            gathers("p1", conv1_t)
            pool.wait_ge(z("conv1_lin"), NCH)
            g.memset(ACCf, 0.0).then_inc(z("acc2_zero"), 1)
            pool.wait_ge(z("conv2_out0"), 64)
            pool.wait_ge(z("conv2_out1"), 48)
            gathers("p2", conv2_t)
            pool.wait_ge(z("xn4_out"), 16 * NCH)
            pool.wait_ge(z("sum_out"), 16 * (NCH + 1))
            network(**FFN)

        @block.scalar
        def _(act):
            a = nc.scalar
            astep = Chain(act, z("a_step"))

            def ln_std(tag, c, s=0):
                act.wait_ge(*norms(tag, "var", c + 1))
                a.activation(SQ[:, s, c * CH:(c + 1) * CH], MV[:, s, c * CH:(c + 1) * CH, 1], ACT.Sqrt,
                             bias=EPSC).then_inc(norms(tag, "std")[0], 1)

            def ln_apply(tag, c, src, dst_, s=0):
                act.wait_ge(*norms(tag, "scale", c + 1))
                for i in range(CH):
                    t = c * CH + i
                    ins = a.activation(dst_(i), src(i), ACT.Identity, bias=NB[:, s, t:t + 1], scale=RS[:, s, t:t + 1])
                ins.then_inc(norms(tag, "norm")[0], 1)

            for c in range(NCH + 1):
                if c < NCH:
                    ln_std("ln0", c)
                if c >= 1:
                    ln_apply("ln0", c - 1, lambda i: X[:, (c - 1) * CH + i, :], lambda i: XN[:, (c - 1) * CH + i, :])
            act.wait_ge(z("edges_f"), 1)
            act.wait_ge(z("small_set"), 1)
            for b in range(1, T):
                astep(a.activation(CMPS[0:EP, :], SRCF[0:EP, :], ACT.Sign, bias=SGN[0:EP, b - 1:b], scale=-1.0,
                                   accum_out=CNT[0:EP, 52 + b:53 + b]))

            def onehot_t(i, j, wait_free):
                act.wait_ge(z("m_tr"), i + 1)
                if wait_free:
                    act.wait_ge(z("m_mm"), i - 1)
                a.copy(OHT[:, j % 2, :], ps[j % 2][:, 0:P]).then_inc(z("m_oht"), 1)
            onehot_t(0, 0, False)

            def message_body(i0, first):
                for u in range(U):
                    i = i0 + u
                    onehot_t(i + 1, u + 1, not (first and u < 1))
                    act.wait_ge(z("m_mm"), i + 1)
                    if not first:
                        act.wait_ge(z(f"ring_dma{u}"), i0)
                    a.copy(G[:, u, 0:D], ps[3 + u % 2][:, 0:D]).then_inc(z("m_row"), 1)
            message_body(0, True)
            with act.Fori(U, NI, U) as i0:
                message_body(i0, False)
            message_loads(act, ACT_, 1)


            def inv_root(tag, y):
                act.wait_ge(z(f"{tag}_y"), 1)
                a.activation(SQ[:, 0, :], y, ACT.Sqrt).then_inc(z(f"{tag}_root"), 1)

            def network(tag, tiles, tiles_before, bias, gelu, **_):
                def hidden(j, e, first):
                    act.wait_ge(z("net_htr"), j + 1 + tiles_before)
                    if not first:
                        act.wait_ge(z("net_mm2"), j + tiles_before)
                    for k in range(HC):
                        col = bias + k if e is None else e * HC + (bias + k)
                        ins = a.activation(HTS[:, k, :], ps[3 + k // 4][:, k % 4 * P:(k % 4 + 1) * P], gelu,
                                           bias=PT[:, bass.ds(col, 1)])
                    ins.then_inc(z("net_gelu"), 1)

                def e_(j):
                    return expert(ACT_, j) if tag == "moe" else None
                act.wait_ge(z("slots"), 1 + (tag == "ffn"))
                hidden(0, e_(0), True)
                hidden(1, e_(1), False)
                with act.Fori(2, tiles, 2) as j0:
                    for s in range(2):
                        hidden(j0 + s, e_(j0 + s), False)

            def staging(tag):
                def body(i0, first):
                    for h in range(0, U, 8):
                        if not first:
                            for u in range(h, h + 8):
                                act.wait_ge(z(f"ring_dma{u}"), i0 + BEFORE[tag])
                        a.copy(STG[:, h:h + 8], SRCI[:, bass.ds(i0 + h, 8)]).then_inc(z(f"{tag}_stg"), 8)
                body(0, True)
                with act.Fori(U, NI, U) as i0:
                    body(i0, False)

            inv_root("do", DI)
            for c in range(NCH + 3):
                if c < NCH:
                    ln_std("ln1", c)
                if 1 <= c <= NCH:
                    ln_apply("ln1", c - 1, lambda i: X[:, (c - 1) * CH + i, :], lambda i: ACC[:, (c - 1) * CH + i, 0:D])
                if 2 <= c <= NCH + 1:
                    ln_std("ln2", c - 2, 1)
                if c >= 3:
                    if c >= 5:
                        act.wait_ge(z(f"xn2_out{(c - 3) % 2}"), 16 * ((c - 3) // 2))
                    ln_apply("ln2", c - 3, lambda i: ACC[:, (c - 3) * CH + i, 0:D], lambda i: XR[:, (c - 3) % 2, i, :], 1)
            act.wait_ge(z("logits_set"), 1)
            a.activation(PR, LG, ACT.Exp).then_inc(z("exp_set"), 1)
            network(**MOE)
            for c in range(NCH + 1):
                if c < NCH:
                    ln_std("ln3", c)
                if c >= 1:
                    if c >= 3:
                        act.wait_ge(z(f"conv1_out{(c - 1) % 2}"), 16 * ((c - 1) // 2))
                    ln_apply("ln3", c - 1, lambda i: X[:, (c - 1) * CH + i, :], lambda i: XR[:, (c - 1) % 2, i, :])
            staging("p1")
            inv_root("di", RM)
            for t in range(T):
                c = t // CH
                act.wait_ge(z("lin1"), t + 1)
                if c >= 2 and t % CH == 0:
                    act.wait_ge(z(f"conv2_out{c % 2}"), 16 * (c // 2))
                a.activation(XR[:, c % 2, t % CH, :], ZB[:, t % 2, :], ACT.Relu, scale=DO[:, t:t + 1]
                             ).then_inc(z("relu1"), 1)
            staging("p2")
            for c in range(NCH + 1):
                if c < NCH:
                    ln_std("ln5", c)
                if c >= 1:
                    ln_apply("ln5", c - 1, *[lambda i: ACC[:, (c - 1) * CH + i, 0:D]] * 2)
            for c in range(NCH + 1):
                if c < NCH:
                    ln_std("ln4", c, 1)
                if c >= 1:
                    ln_apply("ln4", c - 1, lambda i: X[:, (c - 1) * CH + i, :], lambda i: ACC[:, (c - 1) * CH + i, 0:D], 1)
            network(**FFN)

        @block.vector
        def _(v):
            step = Chain(v, z("v_step"))

            def ln_stats(tag, c, src_, s=0):
                if c:
                    v.wait_ge(*norms(tag, "var", c))
                for i in range(CH):
                    ins = v.bn_stats(MV6[:, s, i, :], src_(i))
                step(ins)
                for i in range(CH):
                    ins = v.bn_aggr(MV[:, s, c * CH + i, :], MV6[:, s, i, :])
                ins.then_inc(norms(tag, "var")[0], 1)

            def newton(r, t, y, add):
                step(v.scalar_tensor_tensor(t, y, add, r, ALU.add, ALU.mult))
                step(v.tensor_tensor(t, t, r, ALU.mult))
                step(v.tensor_scalar(t, t, -0.5, 1.5, ALU.mult, ALU.add))
                step(v.tensor_tensor(r, r, t, ALU.mult))

            def ln_scale(tag, c, s=0, extra=None):
                w_ = slice(c * CH, (c + 1) * CH)
                r, n = RS[:, s, w_], NB[:, s, w_]
                v.wait_ge(*norms(tag, "std", c + 1))
                v.wait_ge(*norms(tag, "var", c + 1))
                step(v.reciprocal(r, SQ[:, s, w_]))
                newton(r, T1[:, 0:CH], MV[:, s, w_, 1], EPS)
                if extra is not None:
                    step(v.tensor_tensor(r, r, extra[:, w_], ALU.mult))
                v.scalar_tensor_tensor(n, MV[:, s, w_, 0], -1.0, r, ALU.mult, ALU.mult).then_inc(norms(tag, "scale")[0], 1)

            v.memset(X[96:P, T - 1, :], 0.0)
            v.memset(DSTR[0:P, EC:EC + 1], int(FAR))
            v.memset(PADM[:, 0:W - 1], 0.0)
            v.memset(PADM[:, W - 1:W], -FAR)
            v.memset(PADR[0:1, 0:P], -int(FAR))
            v.memset(PT[:], 0.0)
            step(v.memset(PADR[0:1, P:3 * P], 0))
            v.engine_nop().then_inc(z("pads_set"), 1)
            v.memset(EPSC, EPS)
            v.memset(etab[0:1, :], 0)
            v.memset(ZEROC, 0.0)
            v.memset(ZERO, 0.0)
            v.memset(CNT, 0.0)
            v.wait_ge(z("const"), 7)
            v.tensor_copy(TRIB[:, 0, :], TRI[:])
            v.tensor_scalar(TRIB[:, 1, :], TRI[:], -1.0, 1.0, ALU.mult, ALU.add)
            v.tensor_scalar(SGN, IOTA[:, 1:T], float(P), -0.5, ALU.mult, ALU.add).then_inc(z("small_set"), 1)
            v.wait_ge(z("edges_in"), 48)
            v.tensor_copy(DSTF[0:EP, 0:EC + 1], DSTR[0:EP, 0:EC + 1])
            v.tensor_copy(SRCF[0:EP, :], SRCR[0:EP, :]).then_inc(z("edges_f"), 1)
            for c in range(NCH + 1):
                if c < NCH:
                    v.wait_ge(z(f"x_in{c}"), 16 * (1 + (c == NCH - 1)))
                    ln_stats("ln0", c, lambda i: X[:, c * CH + i, :])
                if c >= 1:
                    ln_scale("ln0", c - 1)
            v.wait_ge(z("edges_f"), 1)
            for b in range(1, T):
                step(v.tensor_scalar(CMPD[0:EP, :], DSTF[0:EP, 0:EC], float(b * P), None, ALU.is_lt, ALU.add,
                                     accum_out=CNT[0:EP, b:b + 1]))
            v.scalar_tensor_tensor(CMPD[0:EP, :], DSTF[0:EP, 0:EC], 0.0, DSTF[0:EP, 1:EC + 1], ALU.add, ALU.is_gt,
                                   accum_out=CNT[0:EP, 50:51]).then_inc(z("counted_d"), 1)

            def attributes(tot, mult, add, keep_starts=False):
                st, hi, lo = ST[:, 0:T + 1], ST[:, 1:T + 1], ST[:, 0:T]
                step(v.tensor_scalar(st, tot, mult, add, ALU.mult, ALU.add))
                v.memset(ST[:, 0:1], 0.0)
                step(v.memset(ST[:, T:T + 1], float(E)))
                if keep_starts:
                    step(v.tensor_copy(STS[:, 0:T + 1], st))
                step(v.tensor_copy(STI[:, 0:T + 1], st))
                step(v.tensor_scalar(STI[:, 0:T + 1], STI[:, 0:T + 1], 7, None, ALU.arith_shift_right))
                step(v.tensor_copy(BLF[:, 0:T + 1], STI[:, 0:T + 1]))
                step(v.tensor_scalar(TJ[:, 0:T], hi, 1.0, None, ALU.subtract))
                step(v.tensor_copy(STI[:, 0:T], TJ[:, 0:T]))
                step(v.tensor_scalar(STI[:, 0:T], STI[:, 0:T], 7, None, ALU.arith_shift_right))
                step(v.tensor_copy(ENF[:, 0:T], STI[:, 0:T]))
                step(v.tensor_tensor(TJ[:, 0:T], hi, lo, ALU.is_gt))
                step(v.scalar_tensor_tensor(NB49[:, 0:T], ENF[:, 0:T], 1.0, BLF[:, 0:T], ALU.add, ALU.subtract))
                step(v.tensor_tensor(NB49[:, 0:T], NB49[:, 0:T], TJ[:, 0:T], ALU.mult))
                step(v.tensor_tensor_scan(INCL[:, 0:T], ONES[:, 0:T], NB49[:, 0:T], 0.0, ALU.mult, ALU.add))
                step(v.tensor_tensor(OFF[:, 0:T], INCL[:, 0:T], NB49[:, 0:T], ALU.subtract))
                step(v.tensor_tensor(KK[:, 0:T], BLF[:, 0:T], OFF[:, 0:T], ALU.subtract))
                step(v.tensor_tensor(DK[:, 0:T - 1], KK[:, 1:T], KK[:, 0:T - 1], ALU.subtract))
                for k in range(NIT):
                    v.tensor_scalar(JUNK[:, 0:T - 1], OFF[:, 1:T], J7[:, k:k + 1], None, ALU.is_le, ALU.add,
                                    accum_out=BSEL[:, k:k + 1])
                    step(v.scalar_tensor_tensor(TJ[:, 0:T - 1], OFF[:, 1:T], J7[:, k:k + 1], DK[:, 0:T - 1],
                                                ALU.is_le, ALU.mult, accum_out=KSL[:, k:k + 1]))
                step(v.tensor_copy(ATB, BSEL))
                step(v.tensor_tensor(ATK, KSL, J7, ALU.add))
                step(v.tensor_scalar(ATK, ATK, KK[:, 0:1], float(NBLK - 1), ALU.add, ALU.min))
                step(v.tensor_scalar(ATC, J7, INCL[:, T - 1:T], FAR, ALU.is_ge, ALU.mult))
                step(v.scalar_tensor_tensor(ATC, ATB, float(P), ATC, ALU.mult, ALU.add))

            row_no = [0]

            def to_rows(attr):
                r = row_no[0]
                row_no[0] += 1
                v.tensor_tensor(DG, IDENT[:].rearrange("p (k n) -> p k n", k=1).to_broadcast([P, NIT, P]),
                                attr.rearrange("p (k n) -> p k n", n=1).to_broadcast([P, NIT, P]), ALU.mult
                                ).then_inc(z("diag_set"), 1)
                v.wait_ge(z("row_made"), r + 1)

            def row_out(ops, to):
                ops(to[:, 0:512], ps[1][0:to.shape[0], 0:512])
                ops(to[:, 512:NIP], ps[2][0:to.shape[0], 0:NIP - 512])

            v.wait_ge(z("totals_d"), 1)
            attributes(ps[0][:, 0:T + 1], 1.0, 0.0)
            v.tensor_copy(BLKI, ATK).then_inc(z("blocks_set"), 1)
            to_rows(ATB)
            row_out(lambda o_, i_: v.tensor_scalar(o_, i_, float(D), None, ALU.mult).then_inc(z("row_used"), 1),
                    rows[0:1, ROW_D, :])
            to_rows(ATC)
            row_out(lambda o_, i_: v.tensor_copy(o_, i_).then_inc(z("row_used"), 1), CD)
            v.wait_ge(z("totals_s"), 1)
            attributes(ps[0][:, 52:52 + T + 1], 0.5, E / 2, keep_starts=True)
            v.engine_nop().then_inc(z("starts_set"), 1)
            to_rows(ATB)
            row_out(lambda o_, i_: v.tensor_scalar(o_, i_, float(D + 1), None, ALU.mult).then_inc(z("row_used"), 1),
                    rows[0:1, ROW_SA, :])
            to_rows(ATK)
            row_out(lambda o_, i_: v.tensor_copy(o_, i_).then_inc(z("row_used"), 1), rows[0:1, ROW_SB, :])
            to_rows(ATC)
            row_out(lambda o_, i_: v.tensor_copy(o_, i_).then_inc(z("row_used"), 1), CS)
            v.wait_ge(z("row_used"), 10)
            v.engine_nop().then_inc(z("rows_set"), 5)
            for k in range(NIT):
                v.wait_ge(z("rec_out"), 16 * NIT)
                v.tensor_copy(RF[:, k, :, :], recs[:, k, 0:2, :]).then_inc(z("rec_f"), 1)
            for k in range(NIT):
                v.wait_ge(z("rec_t"), k + 1)
                c_ = slice(k * P, (k + 1) * P)
                pk = ps[3 + k % 2]
                v.tensor_tensor(DREL[:, c_], pk[:, 0:P], CD[:, c_], ALU.subtract)
                v.tensor_copy(SB[:, c_], pk[:, P:2 * P])
                v.tensor_copy(WT[:, c_], pk[:, 2 * P:3 * P]).then_inc(z("rec_used"), 1)
            v.wait_ge(z("rec_used"), NIT)
            step(v.tensor_scalar(OUT_OF, DREL, 0.0, None, ALU.is_ge))
            step(v.scalar_tensor_tensor(OUT_OF, DREL, float(P), OUT_OF, ALU.is_lt, ALU.mult))
            step(v.tensor_copy(SRCI, SB))
            HI = DG.rearrange("p k n -> p (k n)").bitcast(I32)
            step(v.tensor_scalar(HI, SRCI, 7, None, ALU.arith_shift_right))
            step(v.tensor_copy(SB, HI))
            step(v.scalar_tensor_tensor(SB, SB, 1.0, OUT_OF, ALU.add, ALU.mult))
            step(v.tensor_scalar(SB, SB, 1.0, None, ALU.subtract))
            step(v.tensor_scalar(OUT_OF, OUT_OF, -FAR, FAR, ALU.mult, ALU.add))

            v.wait_ge(z("msg_pad"), 16)
            v.wait_ge(z("rec_in"), 9 * 16)
            step(v.memset(G[:, :, D:D + 1], 1.0))

            def onehots(i, j, wait_free):
                if wait_free:
                    v.wait_ge(z("m_tr"), i - 3)
                v.tensor_scalar(OH[:, j % 4, :], IOTA[:], DREL[:, bass.ds(i, 1)], WT[:, bass.ds(i, 1)],
                                ALU.is_equal, ALU.mult).then_inc(z("m_oh"), 1)
                v.tensor_scalar(BOH[:, j % 4, 0:T], IOTA[:, 0:T], SB[:, bass.ds(i, 1)], None,
                                ALU.is_equal).then_inc(z("m_boh"), 1)
            onehots(0, 0, False)

            def message_body(i0, first):
                for u in range(U):
                    i = i0 + u
                    onehots(i + 1, u + 1, not (first and u < 3))
                    if u % 8 == 0:
                        if not first:
                            for w_ in range(u, u + 8):
                                v.wait_ge(z(f"ring_dma{w_}"), i0)
                        v.tensor_copy(G[:, u:u + 8, D + 1], SRCI[:, bass.ds(i, 8)]).then_inc(z("m_src"), 8)
                    v.wait_ge(z("m_rank"), i + 1)
                    v.scalar_tensor_tensor(JUNK[:, 0:T], ps[2][:, 0:T], 1.0, BOH[:, u % 4, 0:T], ALU.mult, ALU.mult,
                                           accum_out=POS[:, u % 4:u % 4 + 1]).then_inc(z("m_pos"), 1)
                    v.wait_ge(z("m_pos"), i + 1)
                    if u % 8 == 0:
                        v.wait_ge(z("m_src"), i + 8)
                    v.tensor_scalar(PIDX[:, u:u + 1], POS[:, u % 4:u % 4 + 1], OUT_OF[:, bass.ds(i, 1)], None,
                                    ALU.add).then_inc(z("m_idx"), 1)
            message_body(0, True)
            with v.Fori(U, NI, U) as i0:
                message_body(i0, False)

            v.wait_ge(z("m_mm"), NI)
            v.memset(ACCf[:, 0:ACC_CUT], 0.0).then_inc(z("acc_zero"), 1)
            v.wait_ge(z("acc_zero"), 2)

            def s_onehot(i0, u):
                uu = u % U
                i = i0 + u
                v.wait_ge(z(f"sorted_in{uu}"), i0 + (16 if u < U else 32))
                v.tensor_scalar(OH[:, u % 4, :], IOTA[:], CS[:, bass.ds(i, 1)], G[:, uu, D + 1:D + 2],
                                ALU.add, ALU.is_equal).then_inc(z("s_oh"), 1)
            s_onehot(0, 0)
            s_onehot(0, 1)
            v.engine_nop().then_inc(z("s_add"), 1)

            def sum_body(i0, last):
                for u in range(U):
                    i = i0 + u
                    if u % 4 == 0:
                        offs = load4(DVE_, ROW_SA, i, (T - 1) * (D + 1))
                    if not (last and u + 2 >= U):
                        s_onehot(i0, u + 2)
                    v.wait_ge(z("s_add"), i + 1)
                    v.wait_ge(z("s_mm"), i + 1)
                    acc = ACCf[:, bass.ds(offs[u % 4], D + 1)]
                    v.tensor_tensor(acc, acc, ps[u % 4][:, 0:D + 1], ALU.add).then_inc(z("s_add"), 1)
            with v.Fori(0, NI - U, U) as i0:
                sum_body(i0, False)
            sum_body(NI - U, True)


            def inv_root(tag, r, y):
                v.engine_nop().then_inc(z(f"{tag}_y"), 1)
                v.wait_ge(z(f"{tag}_root"), 1)
                step(v.reciprocal(r, SQ[:, 0, :]))
                newton(r, T1, y, 0.0)

            def invert(tag, tiles, steps, value):
                for n in range(steps):
                    s, t = n // T, n % T
                    if n >= 2:
                        v.wait_ge(z(f"{tag}_inv"), n)
                    v.tensor_scalar(A_OH[:, n % 2, :], IOTA[:], HILO[:, 1, s, t:t + 1], None, ALU.is_equal)
                    v.tensor_scalar(B_OH[:, n % 2, 0:tiles], IOTA[:, 0:tiles], HILO[:, 0, s, t:t + 1],
                                    IDT[:, t:t + 1], ALU.is_equal, ALU.mult)
                    v.tensor_scalar(B_OH[:, n % 2, tiles:2 * tiles], IOTA[:, 0:tiles], HILO[:, 0, s, t:t + 1],
                                    value(s, t), ALU.is_equal, ALU.mult).then_inc(z(f"{tag}_oh"), 1)
                v.wait_ge(z(f"{tag}_inv"), steps + 1)
                r, free = A_OH.rearrange("p s n -> p (s n)")[:, 0:tiles], B_OH.rearrange("p s n -> p (s n)")[:, 0:tiles]
                step(v.tensor_scalar(r, ps[2][:, 0:tiles], 1.0, 0.0, ALU.subtract, ALU.max))
                step(v.tensor_copy(gidx_t[:, 0:tiles], r))
                step(v.tensor_scalar(free, ps[2][:, 0:tiles], 0.0, SC[:, 0:1], ALU.is_equal, ALU.mult))
                step(v.scalar_tensor_tensor(r, ps[2][:, 0:tiles], -1.0, free, ALU.add, ALU.add))
                step(v.tensor_copy(sidx_t[:, 0:tiles], r))
                step(v.tensor_copy(gate_t[:, 0:tiles], ps[2][:, tiles:2 * tiles]))
                v.engine_nop().then_inc(z("slots"), 1)

            def places(pos, n):
                step(v.tensor_copy(TII[:, 0, 0:n, :], pos[:, 0:n, :]))
                step(v.tensor_scalar(TII[:, 1, 0:n, :], TII[:, 0, 0:n, :], P - 1, None, ALU.bitwise_and))
                step(v.tensor_scalar(TII[:, 0, 0:n, :], TII[:, 0, 0:n, :], 7, None, ALU.arith_shift_right))
                step(v.tensor_copy(HILO[:, :, 0:n, :], TII[:, :, 0:n, :]))

            def network(tag, tiles, tiles_before, **_):
                experts = tag == "moe"

                def e_(j):
                    return expert(DVE_, j) if experts else None

                def stage_in(j, s, h0, first):
                    if not first:
                        v.wait_ge(z(f"net_in{s}"), h0 + tiles_before * 8)
                    v.tensor_copy(GIDX[:, s:s + 1], gidx_t[:, bass.ds(j, 1)]).then_inc(z("net_gidx"), 1)

                def normed(j, s, e):
                    v.wait_ge(z("net_tr"), j + 1 + tiles_before)
                    for c in range(KC):
                        i_ = ps[0][:, c * P:(c + 1) * P]
                        if experts:
                            ins = v.tensor_scalar(XE[:, s, c, :], i_, PT[:, bass.ds(e * KC + c, 1)],
                                                  PT[:, bass.ds(e * KC + (NE * KC + c), 1)], ALU.mult, ALU.add)
                        else:
                            ins = v.tensor_copy(XE[:, s, c, :], i_)
                    ins.then_inc(z("net_xe"), 1)

                def hidden(j, first):
                    v.wait_ge(z("net_mm1"), j + 1 + tiles_before)
                    if not first:
                        v.wait_ge(z("net_htr"), j + tiles_before)
                    v.tensor_copy(HS[:, 0:512], ps[1][:, 0:512])
                    v.tensor_copy(HS[:, 512:H], ps[2][:, 0:H - 512]).then_inc(z("net_hs"), 1)

                def result(j, s, e, h0, first):
                    v.wait_ge(z("net_mm2"), j + 1 + tiles_before)
                    if not first:
                        v.wait_ge(z(f"net_added{s}"), h0 + tiles_before * 8)
                    v.tensor_copy(SIDX[:, s:s + 1], sidx_t[:, bass.ds(j, 1)])
                    b_ = B2B[:, bass.ds(e * D, D)] if experts else FB2B
                    v.tensor_tensor(YO[:, s, :], ps[5 + s][:, 0:D], b_, ALU.add).then_inc(z("net_y"), 1)
                    v.wait_ge(z("net_y"), j + 1 + tiles_before)
                    v.tensor_scalar(YO[:, s, :], YO[:, s, :], gate_t[:, bass.ds(j, 1)], None, ALU.mult
                                    ).then_inc(z("net_out"), 1)

                stage_in(0, 0, 0, True)
                stage_in(1, 1, 0, True)
                normed(0, 0, e_(0))
                hidden(0, True)
                normed(1, 1, e_(1))
                stage_in(2, 0, 16, False)
                hidden(1, False)
                normed(2, 0, e_(2))
                stage_in(3, 1, 16, False)
                result(0, 0, e_(0), 0, True)
                def pair(j0, first):
                    h0 = j0 * 8
                    hidden(j0, False)
                    normed(j0 + 1, 1, e_(j0 + 1))
                    stage_in(j0 + 2, 0, h0 + 16, False)
                    result(j0 - 1, 1, e_(j0 - 1), None if first else h0 - 16, first)
                    hidden(j0 + 1, False)
                    normed(j0 + 2, 0, e_(j0 + 2))
                    stage_in(j0 + 3, 1, h0 + 16, False)
                    result(j0, 0, e_(j0), h0, False)
                pair(2, True)
                with v.Fori(4, tiles - 2, 2) as j0:
                    pair(j0, False)
                j0, h0 = tiles - 2, (tiles - 2) * 8
                hidden(j0, False)
                normed(j0 + 1, 1, e_(j0 + 1))
                result(j0 - 1, 1, e_(j0 - 1), h0 - 16, False)
                hidden(j0 + 1, False)
                result(j0, 0, e_(j0), h0, False)
                result(j0 + 1, 1, e_(j0 + 1), h0, False)

            def item_sums(tag):
                def onehot(i, j):
                    v.tensor_scalar(OH[:, j % 4, :], IOTA[:], DREL[:, bass.ds(i, 1)], None, ALU.is_equal
                                    ).then_inc(z(f"{tag}_oh"), 1)

                def body(i0):
                    for u in range(U):
                        i = i0 + u
                        if u % 4 == 0:
                            offs = load4(DVE_, ROW_D, i, (T - 1) * (D + 1))
                        onehot(i + 2, u + 2)
                        v.wait_ge(z(f"{tag}_add"), i + 1)
                        v.wait_ge(z(f"{tag}_mm"), i + 1)
                        acc = ACCf[:, bass.ds(offs[u % 4], D + 1)]
                        v.tensor_tensor(acc, acc, ps[u % 4][:, 0:D + 1], ALU.add).then_inc(z(f"{tag}_add"), 1)
                step(v.memset(G[:, :, D:D + 1], 1.0))
                onehot(0, 0)
                onehot(1, 1)
                v.engine_nop().then_inc(z(f"{tag}_add"), 1)
                with v.Fori(0, NI - U, U) as i0:
                    body(i0)
                body(NI - U)

            def evacuate(tag, t):
                v.wait_ge(z(f"{tag}_tr"), t + 1)
                if t >= 2:
                    v.wait_ge(z(f"{tag}_mm"), t - 1)
                v.tensor_copy(XT[:, t % 2, :, :].rearrange("p c n -> p (c n)"), ps[t % 2][:, 0:D]
                              ).then_inc(z(f"{tag}_xt"), 1)

            v.wait_ge(z("s_add"), NI + 1)
            step(v.tensor_scalar(DI, ACC[:, :, D], 1.0, None, ALU.max))
            inv_root("do", DO, DI)
            v.wait_ge(z("par_in"), PAR_IN)
            for c in range(NCH + 3):
                if c < NCH:
                    w_ = slice(c * CH, (c + 1) * CH)
                    v.tensor_tensor(X[:, w_, :], X[:, w_, :], ACC[:, w_, 0:D], ALU.add).then_inc(z("x1_set"), 1)
                    v.wait_ge(z("x1_set"), c + 1)
                    ln_stats("ln1", c, lambda i: X[:, c * CH + i, :])
                if 1 <= c <= NCH:
                    ln_scale("ln1", c - 1)
                if 2 <= c <= NCH + 1:
                    v.wait_ge(*norms("ln1", "norm", c - 1))
                    ln_stats("ln2", c - 2, lambda i: ACC[:, (c - 2) * CH + i, 0:D], 1)
                    for i in range(CH):
                        evacuate("rt", (c - 2) * CH + i)
                if c >= 3:
                    ln_scale("ln2", c - 3, 1)
            v.wait_ge(z("par_t"), 1)
            step(v.tensor_copy(PT[:], ps[3][:, 0:P]))
            for k, n in ((0, 64), (1, 48)):
                v.wait_ge(z(f"xn2_out{k}"), n)
            v.wait_ge(z("rt_mm"), T)
            l3 = ps[2][:, 0:TE].rearrange("p (t e) -> p t e", e=NE)
            step(v.tensor_tensor(LG3, l3, per_column(BRB[:, 0:NE], T), ALU.add))
            step(v.tensor_reduce(RM, LG3, AX.X, ALU.max))
            step(v.tensor_tensor(LG3, LG3, per_node(RM), ALU.subtract))
            v.engine_nop().then_inc(z("logits_set"), 1)
            v.tensor_scalar(DESC, IOTA[:, 0:NE], -1.0, float(NE), ALU.mult, ALU.add)
            v.memset(VAL, 1.0)
            step(v.tensor_scalar(SC[:, 0:1], PCOL, float(N + 1), None, ALU.add))
            step(v.tensor_scalar(VAL[:, T - 1:T], PCOL, float(LAST), None, ALU.is_lt))
            v.wait_ge(z("exp_set"), 1)
            step(v.tensor_reduce(RM, PR3, AX.X, ALU.add))
            step(v.reciprocal(RM, RM))
            step(v.tensor_tensor(PR3, PR3, per_node(RM), ALU.mult))

            def largest(oh, m):
                step(v.tensor_reduce(m, PR3, AX.X, ALU.max))
                step(v.tensor_tensor(EQ3, PR3, per_node(m), ALU.is_equal))
                step(v.tensor_tensor(EQ3, EQ3, per_column(DESC, T), ALU.mult))
                step(v.tensor_reduce(RM, EQ3, AX.X, ALU.max))
                step(v.tensor_tensor(oh, EQ3, per_node(RM), ALU.is_equal))
            largest(OH1, GT[:, 0, :])
            step(v.scalar_tensor_tensor(PR, OHB[:, 0:TE], -2.0, PR, ALU.mult, ALU.add))
            largest(OH2, GT[:, 1, :])
            step(v.tensor_tensor(RM, GT[:, 0, :], GT[:, 1, :], ALU.add))
            step(v.reciprocal(RM, RM))
            for k, oh in enumerate((OH1, OH2)):
                step(v.tensor_tensor(GT[:, k, :], GT[:, k, :], RM, ALU.mult))
                step(v.tensor_tensor(oh, oh, per_node(VAL), ALU.mult))
            v.tensor_tensor(LG, OHB[:, 0:TE], OHB[:, TE:2 * TE], ALU.add).then_inc(z("choice_set"), 1)
            et = "p (e t) -> p e t"
            v.wait_ge(z("choice_rank"), 1)
            step(v.tensor_copy(EXC.rearrange(et, e=NE), ps[1][:, 0:TE].rearrange("p (t e) -> p e t", e=NE)))
            step(v.memset(EQ, 1.0))
            step(v.tensor_tensor_scan(INC[:, 0:TE], EQ, EXC, 0.0, ALU.mult, ALU.add))
            step(v.tensor_tensor(EXC, INC[:, 0:TE], EXC, ALU.subtract))
            end, start = INC[:, 0:TE].rearrange(et, e=NE)[:, :, T - 1], EXC.rearrange(et, e=NE)[:, :, 0]
            step(v.tensor_tensor(TLN, end, start, ALU.subtract))
            step(v.tensor_scalar(TLN, TLN, float(P - 1), None, ALU.add))
            step(v.tensor_copy(TLI, TLN))
            step(v.tensor_scalar(TLI, TLI, 7, None, ALU.arith_shift_right))
            step(v.tensor_copy(TLN, TLI))
            step(v.tensor_tensor_scan(TOFF, ONES[:, 0:NE], TLN, 0.0, ALU.mult, ALU.add))
            step(v.tensor_tensor(TOFF, TOFF, TLN, ALU.subtract))
            step(v.scalar_tensor_tensor(PB, TOFF, float(P), start, ALU.mult, ALU.subtract))
            r3 = ps[0][:, 0:TE].rearrange("p (t e) -> p t e", e=NE)
            step(v.tensor_tensor(PA, r3, EXC.rearrange("p (e t) -> p t e", e=NE), ALU.add))
            step(v.tensor_tensor(PA, PA, per_column(PB, T), ALU.add))
            for k, oh in enumerate((OH1, OH2)):
                step(v.tensor_tensor(oh, oh, PA, ALU.mult))
                step(v.tensor_reduce(PK[:, k, :], oh, AX.X, ALU.add))
            step(v.tensor_scalar(RM, VAL, -FAR, FAR, ALU.mult, ALU.add))
            for k in range(2):
                step(v.tensor_tensor(PK[:, k, :], PK[:, k, :], RM, ALU.add))
            step(v.tensor_scalar(IDT, IOTA[:, 0:T], float(P), PCOL, ALU.mult, ALU.add))
            step(v.tensor_scalar(IDT, IDT, 1.0, None, ALU.add))
            places(PK, 2)
            ef = A_OH.rearrange("p s n -> p (s n)")[:, 0:NT]
            step(v.tensor_scalar(ef, IOTA[:, 0:NT], TOFF[:, 1:2], None, ALU.is_ge))
            for e in range(2, NE):
                step(v.scalar_tensor_tensor(ef, IOTA[:, 0:NT], TOFF[:, e:e + 1], ef, ALU.is_ge, ALU.add))
            step(v.tensor_copy(etab[0:1, 0:NT], ef[0:1, :]))
            invert("moe", NT, 2 * T, lambda s, t: GT[:, s, t:t + 1])
            network(**MOE)

            for c in range(NCH + 1):
                if c < NCH:
                    v.wait_ge(z(f"x_in{c}"), 16 * (2 + (c == NCH - 1)))
                    ln_stats("ln3", c, lambda i: X[:, c * CH + i, :])
                if c >= 1:
                    ln_scale("ln3", c - 1, extra=DO)
            v.wait_ge(z("acc1_zero"), 1)
            step(v.tensor_scalar(rows[0:1, ROW_D, :], rows[0:1, ROW_D, :], (D + 1) / D, None, ALU.mult))
            for k, n in ((0, 64), (1, 48)):
                v.wait_ge(z(f"conv1_out{k}"), n)
            v.engine_nop().then_inc(z("conv_ready"), 1)
            item_sums("p1")
            v.wait_ge(z("p1_add"), NI + 1)
            step(v.tensor_scalar(RM, ACC[:, :, D], 1.0, None, ALU.max))
            inv_root("di", DI, RM)
            v.wait_ge(z("tail_in"), 8 * 16)

            def product(tag, l, t, to, bias):
                v.wait_ge(z(f"{tag}_mm"), t + 1)
                return v.scalar_tensor_tensor(to, ps[2 + t % 2][:, 0:D], DI[:, t:t + 1], bias, ALU.mult, ALU.add)
            evacuate("c1", 0)
            for t in range(T):
                if t + 1 < T:
                    evacuate("c1", t + 1)
                if t >= 2:
                    v.wait_ge(z("relu1"), t - 1)
                product("c1", 0, t, ZB[:, t % 2, :], GB1B).then_inc(z("lin1"), 1)
            v.engine_nop().then_inc(z("conv1_lin"), NCH)
            v.wait_ge(z("acc2_zero"), 1)
            for k, n in ((0, 64), (1, 48)):
                v.wait_ge(z(f"conv2_out{k}"), n)
            v.engine_nop().then_inc(z("conv_ready"), 1)
            item_sums("p2")
            v.wait_ge(z("p2_add"), NI + 1)
            evacuate("c2", 0)
            for t in range(T):
                if t + 1 < T:
                    evacuate("c2", t + 1)
                product("c2", 1, t, ACC[:, t, 0:D], GB2B).then_inc(z("lin2"), 1)
                if t % CH == CH - 1:
                    v.wait_ge(z("lin2"), t + 1)
                    c = t // CH
                    ln_stats("ln5", c, lambda i: ACC[:, c * CH + i, 0:D])
                    ln_scale("ln5", c)
            for c in range(NCH + 1):
                if c < NCH:
                    w_ = slice(c * CH, (c + 1) * CH)
                    h = ACC[:, w_, 0:D]
                    v.wait_ge(*norms("ln5", "norm", c + 1))
                    step(v.tensor_tensor(h, h, per_column(GAMB, CH), ALU.mult))
                    step(v.tensor_tensor(h, h, per_column(BETB, CH), ALU.add))
                    step(v.tensor_tensor(X[:, w_, :], X[:, w_, :], h, ALU.add))
                    ln_stats("ln4", c, lambda i: X[:, c * CH + i, :], 1)
                if c >= 1:
                    ln_scale("ln4", c - 1, 1)
            for c in range(NCH):
                w_ = slice(c * CH, (c + 1) * CH)
                v.wait_ge(*norms("ln4", "norm", c + 1))
                v.tensor_tensor(X[:, w_, :], X[:, w_, :], ACC[:, w_, 0:D], ALU.add).then_inc(z("sum_set"), 1)
                for t in range(c * CH, (c + 1) * CH):
                    step(v.scalar_tensor_tensor(HS[:, 0:D], ACC[:, t, 0:D], 1.0, FWRB, ALU.mult, ALU.mult,
                                                accum_out=WV[:, t:t + 1]))
            step(v.tensor_scalar(WV, WV, FBR, None, ALU.add))

            ROUND = [0]

            def count(into, scores, bound, op):
                step(v.scalar_tensor_tensor(T1, scores, bound, VAL, op, ALU.mult, accum_out=SC[:, 1:2]))
                v.engine_nop().then_inc(z("cnt_set"), 1)
                ROUND[0] += 1
                v.wait_ge(z("cnt_sum"), ROUND[0])
                return ps[1][:, 0:1]
            THR, CAND, KEEP, SIGN, KTH, NEED = (SC[:, k:k + 1] for k in range(2, 8))
            total = count(None, WV, ZEROC, ALU.is_ge)
            step(v.tensor_scalar(SIGN, total, float(KSEL), None, ALU.is_ge))
            step(v.tensor_scalar(KTH, SIGN, float(2 * KSEL - N - 1), float(N - KSEL + 1), ALU.mult, ALU.add))
            step(v.tensor_scalar(SIGN, SIGN, 2.0, -1.0, ALU.mult, ALU.add))
            step(v.tensor_scalar(RM, WV, SIGN, None, ALU.mult))
            step(v.memset(THR, 0.0))
            for bit in range(30, -1, -1):
                step(v.tensor_scalar(CAND.bitcast(I32), THR.bitcast(I32), 1 << bit, None, ALU.bitwise_or))
                total = count(None, RM, CAND, ALU.is_ge)
                step(v.tensor_scalar(KEEP, total, KTH, 3.0e38, ALU.is_ge, ALU.mult))
                step(v.scalar_tensor_tensor(THR, CAND, KEEP, THR, ALU.min, ALU.max))
            step(v.tensor_scalar(THR, THR, SIGN, None, ALU.mult))
            total = count(None, WV, THR, ALU.is_gt)
            step(v.tensor_scalar(NEED, total, -1.0, float(KSEL), ALU.mult, ALU.add))
            step(v.scalar_tensor_tensor(EQ[:, 0:T], WV, THR, VAL, ALU.is_equal, ALU.mult))

            def prefix(n):
                v.engine_nop().then_inc(z("mark_set"), 1)
                v.wait_ge(z("mark_rank"), n)
                step(v.tensor_copy(EXC[:, 0:T], ps[1][:, 64:64 + T]))
                step(v.tensor_tensor_scan(INC[:, 0:T], ONES[:, 0:T], EXC[:, 0:T], 0.0, ALU.mult, ALU.add))
                step(v.tensor_tensor(EXC[:, 0:T], INC[:, 0:T], EXC[:, 0:T], ALU.subtract))
                step(v.tensor_tensor(EXC[:, 0:T], EXC[:, 0:T], ps[0][:, 0:T], ALU.add))
                return EXC[:, 0:T]
            r = prefix(1)
            step(v.scalar_tensor_tensor(RM, r, NEED, EQ[:, 0:T], ALU.is_lt, ALU.mult))
            step(v.scalar_tensor_tensor(T1, WV, THR, VAL, ALU.is_gt, ALU.mult))
            step(v.tensor_tensor(EQ[:, 0:T], RM, T1, ALU.add))
            r = prefix(2)
            step(v.tensor_scalar(IDT, IOTA[:, 0:T], float(P), PCOL, ALU.mult, ALU.add))
            step(v.scalar_tensor_tensor(RM, IDT, float(KSEL), r, ALU.add, ALU.subtract))
            step(v.tensor_tensor(T1, r, RM, ALU.subtract))
            step(v.tensor_tensor(T1, T1, EQ[:, 0:T], ALU.mult))
            step(v.tensor_tensor(T1, T1, RM, ALU.add))
            step(v.tensor_scalar(RM, VAL, -FAR, FAR, ALU.mult, ALU.add))
            step(v.tensor_tensor(PK[:, 0, :], T1, RM, ALU.add))
            step(v.tensor_tensor(WV, WV, EQ[:, 0:T], ALU.mult))
            step(v.tensor_scalar(IDT, IDT, 1.0, None, ALU.add))
            places(PK, 1)
            invert("ffn", NFT, T, lambda s, t: WV[:, t:t + 1])
            v.wait_ge(z("sum_out"), 16 * (NCH + 1))
            network(**FFN)

        @block.tensor
        def _(pe):
            def totals(c, at, tag):
                if tag == "d":
                    pe.wait_ge(z("counted_d"), 1)
                else:
                    pe.wait_ge(z("a_step"), T - 1)
                pe.matmul(ps[0][:, at:at + 52], ONES[:], CNT[:, at:at + 52], start=True, stop=True
                          ).then_inc(z(f"totals_{tag}"), 1)
            row_no = [0]

            def rows_of():
                r = row_no[0]
                row_no[0] += 1
                pe.wait_ge(z("diag_set"), r + 1)
                if r:
                    pe.wait_ge(z("row_used"), 2 * r)
                d = DG.rearrange("p k n -> p (k n)")
                pe.matmul(ps[1][:, 0:512], ONES[:], d[:, 0:512], start=True, stop=True)
                pe.matmul(ps[2][:, 0:NIP - 512], ONES[:], d[:, 512:NIP], start=True, stop=True
                          ).then_inc(z("row_made"), 1)
            pe.wait_ge(z("const"), CONST)
            totals("d", 0, "d")
            rows_of()
            rows_of()
            totals("s", 52, "s")
            rows_of()
            rows_of()
            rows_of()
            for k in range(NIT):
                pe.wait_ge(z("rec_f"), k + 1)
                if k >= 2:
                    pe.wait_ge(z("rec_used"), k - 1)
                for a_ in range(3):
                    src_ = RF[:, k, a_, :] if a_ < 2 else recs[:, k, 2, :].bitcast(F32)
                    ins = pe.transpose(ps[3 + k % 2][:, a_ * P:(a_ + 1) * P], src_, IDENT[:])
                ins.then_inc(z("rec_t"), 1)

            def transpose_oh(i, j, wait_free):
                pe.wait_ge(z("m_oh"), i + 1)
                if wait_free:
                    pe.wait_ge(z("m_oht"), i - 1)
                pe.transpose(ps[j % 2][:, 0:P], OH[:, j % 4, :], IDENT[:]).then_inc(z("m_tr"), 1)
            pe.wait_ge(z("starts_set"), 1)
            pe.wait_ge(z("row_used"), 10)
            pe.matmul(ps[2][:, 0:T], ONES[0:1, :], STS[0:1, 0:T], start=True, stop=False, skip_group_check=True)
            pe.wait_ge(z("rec_used"), NIT)
            transpose_oh(0, 0, False)

            def rank(i, j, which, note):
                ins = pe.matmul(ps[2][:, 0:T], TRIB[:, which, :], BOH[:, j % 4, 0:T], start=False, stop=False,
                                skip_group_check=True)
                if note:
                    ins.then_inc(z("m_rank"), 1)
            pe.wait_ge(z("m_boh"), 1)
            rank(0, 0, 0, True)
            pe.wait_ge(*norms("ln0", "norm", NCH))

            def message_body(i0, first):
                for u in range(U):
                    i = i0 + u
                    if u % 4 == 0:
                        offs = load4(PE_, ROW_D, i, (T - 1) * D)
                    transpose_oh(i + 1, u + 1, not (first and u < 1))
                    pe.wait_ge(z("m_pos"), i + 1)
                    rank(i, u, 1, False)
                    pe.wait_ge(z("m_boh"), i + 2)
                    rank(i + 1, u + 1, 0, True)
                    pe.wait_ge(z("m_oht"), i + 1)
                    if not (first and u < 2):
                        pe.wait_ge(z("m_row"), i - 1)
                    pe.matmul(ps[3 + u % 2][:, 0:D], OHT[:, u % 2, :], XNf[:, bass.ds(offs[u % 4], D)],
                              start=True, stop=True).then_inc(z("m_mm"), 1)
            pe.wait_ge(z("rows_set"), 5)
            message_body(0, True)
            with pe.Fori(U, NI, U) as i0:
                message_body(i0, False)

            def sum_body(i0, first):
                for u in range(U):
                    i = i0 + u
                    pe.wait_ge(z("s_oh"), i + 1)
                    pe.wait_ge(z(f"sorted_in{u}"), i0 + 16)
                    if not (first and u < 4):
                        pe.wait_ge(z("s_add"), i - 2)
                    pe.matmul(ps[u % 4][:, 0:D + 1], OH[:, u % 4, :], G[:, u, 0:D + 1], start=True, stop=True
                              ).then_inc(z("s_mm"), 1)
            sum_body(0, True)
            with pe.Fori(U, NI, U) as i0:
                sum_body(i0, False)

            def tile_products(tag, t, width, rhs, bank, at, between=None):
                def transposes(t_):
                    if t_ >= 2:
                        pe.wait_ge(z(f"{tag}_xt"), t_ - 1)
                    for c in range(KC):
                        ins = pe.transpose(ps[t_ % 2][:, c * P:(c + 1) * P], ACC[:, t_, c * P:(c + 1) * P], IDENT[:])
                    ins.then_inc(z(f"{tag}_tr"), 1)
                if t == 0:
                    transposes(0)
                if t + 1 < T:
                    if between is not None:
                        between(t + 1)
                    transposes(t + 1)
                pe.wait_ge(z(f"{tag}_xt"), t + 1)
                for c in range(KC):
                    ins = pe.matmul(ps[bank][:, at:at + width], XT[:, t % 2, c, :], rhs(c), start=(c == 0),
                                    stop=(c == KC - 1))
                ins.then_inc(z(f"{tag}_mm"), 1)

            def network(tag, tiles, tiles_before, **_):
                experts = tag == "moe"

                def e_(j):
                    return expert(PE_, j) if experts else None

                def transposes(j, s, h0, first):
                    pe.wait_ge(z(f"net_in{s}"), h0 + tiles_before * 8)
                    if not first:
                        pe.wait_ge(z("net_xe"), j + tiles_before)
                    for c in range(KC):
                        ins = pe.transpose(ps[0][:, c * P:(c + 1) * P], GX[:, s, c * P:(c + 1) * P], IDENT[:])
                    ins.then_inc(z("net_tr"), 1)

                def product1(j, s, e, first):
                    pe.wait_ge(z("net_xe"), j + 1 + tiles_before)
                    if not first:
                        pe.wait_ge(z("net_hs"), j + tiles_before)
                    for h in range(0, H, 512):
                        for c in range(KC):
                            w_ = (w1f[:, bass.ds(e * (KC * H) + (c * H + h), 512)] if experts
                                  else fw1s[:, c, h:h + 512])
                            ins = pe.matmul(ps[1 + h // 512][:, :], XE[:, s, c, :], w_, start=(c == 0),
                                            stop=(c == KC - 1))
                    ins.then_inc(z("net_mm1"), 1)

                def product2(j, s, e, first):
                    pe.wait_ge(z("net_gelu"), j + 1 + tiles_before)
                    if not first:
                        pe.wait_ge(z("net_y"), j - 1 + tiles_before)
                    for k in range(HC):
                        w_ = w2ff[:, bass.ds(e * (HC * D) + k * D, D)] if experts else fw2s[:, k, :]
                        ins = pe.matmul(ps[5 + s][:, 0:D], HTS[:, k, :], w_, start=(k == 0), stop=(k == HC - 1))
                    ins.then_inc(z("net_mm2"), 1)

                def hidden_t(j, first):
                    pe.wait_ge(z("net_hs"), j + 1 + tiles_before)
                    if not first:
                        pe.wait_ge(z("net_gelu"), j + tiles_before)
                    for k in range(HC):
                        ins = pe.transpose(ps[3 + k // 4][:, k % 4 * P:(k % 4 + 1) * P], HS[:, k * P:(k + 1) * P],
                                           IDENT[:])
                    ins.then_inc(z("net_htr"), 1)

                pe.wait_ge(z("slots"), 1 + (not experts))
                transposes(0, 0, 16, True)
                product1(0, 0, e_(0), True)
                transposes(1, 1, 16, False)
                hidden_t(0, True)
                product1(1, 1, e_(1), False)
                transposes(2, 0, 32, False)
                product2(0, 0, e_(0), True)
                hidden_t(1, False)
                def pair(j0, first):
                    h0 = j0 * 8
                    product1(j0, 0, e_(j0), False)
                    transposes(j0 + 1, 1, h0 + 16, False)
                    product2(j0 - 1, 1, e_(j0 - 1), first)
                    hidden_t(j0, False)
                    product1(j0 + 1, 1, e_(j0 + 1), False)
                    transposes(j0 + 2, 0, h0 + 32, False)
                    product2(j0, 0, e_(j0), False)
                    hidden_t(j0 + 1, False)
                pair(2, True)
                with pe.Fori(4, tiles - 2, 2) as j0:
                    pair(j0, False)
                j0, h0 = tiles - 2, (tiles - 2) * 8
                product1(j0, 0, e_(j0), False)
                transposes(j0 + 1, 1, h0 + 16, False)
                product2(j0 - 1, 1, e_(j0 - 1), False)
                hidden_t(j0, False)
                product1(j0 + 1, 1, e_(j0 + 1), False)
                product2(j0, 0, e_(j0), False)
                hidden_t(j0 + 1, False)
                product2(j0 + 1, 1, e_(j0 + 1), False)

            def inversion(tag, tiles, steps):
                pe.matmul(ps[2][:, 0:2 * tiles], ONES[0:1, :], ZERO[0:1, 0:2 * tiles], start=True, stop=False,
                          skip_group_check=True).then_inc(z(f"{tag}_inv"), 1)
                for n in range(steps):
                    pe.wait_ge(z(f"{tag}_oh"), n + 1)
                    pe.matmul(ps[2][:, 0:2 * tiles], A_OH[:, n % 2, :], B_OH[:, n % 2, 0:2 * tiles], start=False,
                              stop=(n == steps - 1), skip_group_check=True).then_inc(z(f"{tag}_inv"), 1)

            def item_products(tag):
                def body(i0, first):
                    for u in range(U):
                        i = i0 + u
                        pe.wait_ge(z(f"{tag}_oh"), i + 1)
                        pe.wait_ge(z(f"ring_dma{u}"), i0 + (16 + BEFORE[tag]))
                        if not (first and u < 4):
                            pe.wait_ge(z(f"{tag}_add"), i - 2)
                        pe.matmul(ps[u % 4][:, 0:D + 1], OH[:, u % 4, :], G[:, u, 0:D + 1], start=True, stop=True
                                  ).then_inc(z(f"{tag}_mm"), 1)
                body(0, True)
                with pe.Fori(U, NI, U) as i0:
                    body(i0, False)

            pe.wait_ge(z("par_in"), PAR_IN)
            pe.wait_ge(z("s_add"), NI + 1)
            pe.transpose(ps[3][:, 0:P], PT[:], IDENT[:]).then_inc(z("par_t"), 1)
            pe.wait_ge(*norms("ln1", "norm", 1))
            for t in range(T):
                def normed(t_):
                    pe.wait_ge(*norms("ln1", "norm", t_ // CH + 1))
                tile_products("rt", t, NE, lambda c: WRS[:, c, :], 2, t * NE, normed)
            pe.wait_ge(z("choice_set"), 1)
            pe.matmul(ps[0][:, 0:TE], TRI[:], LG, start=True, stop=True)
            pe.matmul(ps[1][:, 0:TE], ONES[:], LG, start=True, stop=True).then_inc(z("choice_rank"), 1)
            inversion("moe", NT, 2 * T)
            pe.wait_ge(z("w1_in"), 16 * NE)
            pe.wait_ge(z("w2_in"), 16 * NE)
            network(**MOE)
            pe.wait_ge(z("conv_ready"), 1)
            item_products("p1")
            pe.wait_ge(z("tail_in"), 8 * 16)
            pe.wait_ge(z("p1_add"), NI + 1)
            for t in range(T):
                if t >= 2:
                    pe.wait_ge(z("lin1"), t - 1)
                tile_products("c1", t, D, lambda c: gws[:, 0, c, :], 2 + t % 2, 0)
            pe.wait_ge(z("conv_ready"), 2)
            item_products("p2")
            pe.wait_ge(z("p2_add"), NI + 1)
            for t in range(T):
                if t >= 2:
                    pe.wait_ge(z("lin2"), t - 1)
                tile_products("c2", t, D, lambda c: gws[:, 1, c, :], 2 + t % 2, 0)
            for n in range(1 + 31 + 1):
                pe.wait_ge(z("cnt_set"), n + 1)
                pe.matmul(ps[1][:, 0:1], ONES[:], SC[:, 1:2], start=True, stop=True).then_inc(z("cnt_sum"), 1)
            for n in range(2):
                pe.wait_ge(z("mark_set"), n + 1)
                pe.matmul(ps[0][:, 0:T], TRI[:], EQ[:, 0:T], start=True, stop=True)
                pe.matmul(ps[1][:, 64:64 + T], ONES[:], EQ[:, 0:T], start=True, stop=True).then_inc(z("mark_rank"), 1)
            inversion("ffn", NFT, T)
            pe.wait_ge(z("fw_in"), 32)
            network(**FFN)


_INS = ['x', 'src', 'dst', 'edge_weight', 'L0_ffn_Wr', 'L0_ffn_br', 'L0_ffn_ln_g', 'L0_ffn_ln_b', 'L0_ffn_W1',
        'L0_ffn_b1', 'L0_ffn_W2', 'L0_ffn_b2', 'L1_gnn_W1', 'L1_gnn_b1', 'L1_gnn_W2', 'L1_gnn_b2', 'L1_gnn_gamma',
        'L1_gnn_beta', 'L1_ffn_wr', 'L1_ffn_br', 'L1_ffn_w1', 'L1_ffn_b1', 'L1_ffn_w2', 'L1_ffn_b2']


def kernel(**inputs):
    import numpy as _np
    import concourse.bacc as _bacc
    from concourse import mybir as _mybir
    from concourse.bass_utils import run_bass_kernel_spmd as _run

    nc = _bacc.Bacc("TRN2", target_bir_lowering=False, num_devices=1)
    arrays, args = {}, []
    for name in _INS:
        a = _np.ascontiguousarray(inputs[name])
        arrays[f"in_{name}_dram"] = a
        args.append(nc.dram_tensor(f"in_{name}_dram", a.shape, _mybir.dt.from_np(a.dtype), kind="ExternalInput").ap())
    shape = inputs["x"].shape
    args.append(nc.dram_tensor("out_0_dram", shape, _mybir.dt.from_np(_np.dtype("float32")),
                               kind="ExternalOutput").ap())
    gnn_program(nc, *args)
    r = _run(nc, [arrays], core_ids=[0])
    return r.results[0]["out_0_dram"]
```

```python
from contextlib import ExitStack

import concourse.bass as bass
from concourse import mybir

P = 128
ALU = mybir.AluOpType
ACT = mybir.ActivationFunctionType
F32 = mybir.dt.float32
BF16 = mybir.dt.bfloat16
I32 = mybir.dt.int32
I16 = mybir.dt.int16
AX = mybir.AxisListType
FAR = 1.0e6
EPS = 1.0e-5
IN_RANGE = "computed on the chip from counts, within its range for any input"


class Chain:

    def __init__(self, engine, sem):
        self.engine, self.sem, self.n, self.loop, self.k = engine, sem, 0, None, 0

    def __call__(self, instruction):
        instruction.then_inc(self.sem, 1)
        if self.loop is None:
            self.n += 1
            self.engine.wait_ge(self.sem, self.n)
        else:
            self.k += 1
            it, first, per = self.loop
            self.engine.wait_ge(self.sem, (it - first) * per + (self.n + self.k))

    def enter(self, it, first, per):
        self.loop, self.k = (it, first, per), 0

    def leave(self, rounds):
        _, _, per = self.loop
        assert self.k == per, (self.k, per)
        self.n += rounds * per
        self.loop = None


def gnn_program(nc, x, src, dst, edge_weight, Wr, br, ln_g, ln_b, W1, b1, W2, b2,
                gW1, gb1, gW2, gb2, gamma, beta, fwr, fbr, fw1, fb1, fw2, fb2, out):
    N, D = x.shape
    E = src.shape[0]
    NE, H = W1.shape[0], W1.shape[2]
    T = -(-N // P)
    LAST = N - (T - 1) * P
    KC = D // P
    HC = H // P
    NBLK = -(-E // P)
    TAIL = E - (NBLK - 1) * P
    U = 16
    NI = -(-(NBLK + T - 1) // U) * U
    ROUNDS = NI // U
    assert U == 16
    NIS = -(-(NBLK + 2 * T - 1) // U) * U
    NIT = -(-NIS // P)
    NIP = NIT * P
    W = D + 2
    EP = 125
    EC = E // EP
    assert EP * EC == E and EP < P
    CH = 7
    NCH = T // CH
    assert CH * NCH == T
    NT = (2 * N - NE) // P + NE
    NT += NT % 2
    KSEL = max(1, N // 2) - 1
    NF = -(-KSEL // P)
    FLAST = KSEL - (NF - 1) * P
    FPAD = T * P + P

    with ExitStack() as ctx:
        def sb(name, shape, dt=F32):
            return ctx.enter_context(nc.sbuf_tensor(name, shape, dt))

        def sem(name):
            return ctx.enter_context(nc.semaphore(name))

        def dram(name, shape, dt=F32):
            return nc.dram_tensor(name, shape, dt).ap()

        raw = dram("edges_as_given", [NBLK, 3, P], I32)
        rec = dram("edge_blocks", [NBLK, 3, P], I32)
        msgs = dram("messages", [(NBLK + 1) * P, W])
        xn2_t = dram("expert_in_rows", [T * P, D])
        x2_t = dram("residual_rows", [FPAD, D])
        conv1_t = dram("conv1_rows", [T * P, D])
        conv2_t = dram("conv2_rows", [T * P, D])
        xn4_t = dram("ffn_in_rows", [T * P, D])

        WORK = 4900
        SMALL = 2260
        reg_a = sb("reg_a", [P, NE * KC * H])
        reg_b = sb("reg_b", [P, NE * HC * D])
        tables = sb("tables", [P, 6 * NIP])
        work = sb("work", [P, WORK])
        small = sb("small", [P, SMALL])
        IOTA = sb("iota", [P, P])
        IDENT = sb("ident", [P, P])
        ONES = sb("ones", [P, P])
        TRI = sb("tri", [P, P])
        TRIB = sb("trib", [P, 2, P], BF16)
        PT = sb("param_t", [P, P])
        WRS = sb("wrs", [P, KC, NE])
        B2B = sb("b2_rows", [P, NE * D])
        BRB = sb("brb", [P, NE + 1])
        rows = sb("rows", [1, 3, NIP], I16)
        etab = sb("etab", [1, NT + 4], I32)
        slot_t = sb("slot_t", [P, 3 * (NT + 2)])

        X = reg_a[:, 0:T * D].rearrange("p (t d) -> p t d", d=D)
        w1s = reg_a[:, :].rearrange("p (e c h) -> p e c h", e=NE, c=KC)
        XNf = reg_b[:, 0:T * D]
        XN = XNf.rearrange("p (t d) -> p t d", d=D)
        ACCf = reg_b[:, 0:T * (D + 1)]
        ACC = ACCf.rearrange("p (t d) -> p t d", d=D + 1)
        w2s = reg_b[:, :].rearrange("p (e c d) -> p e c d", e=NE, c=HC)
        w1f, w2ff = reg_a[:, :], reg_b[:, :]
        recs = reg_b[:, T * D:T * D + NIT * 3 * P].bitcast(I32).rearrange("p (k a j) -> p k a j", k=NIT, a=3)
        ta = reg_a[:, T * D:]
        DG = ta[:, 0:NIP].rearrange("p (k n) -> p k n", n=P)
        RF = ta[:, NIP:NIP + NIT * 2 * P].rearrange("p (k a j) -> p k a j", k=NIT, a=2)
        CD = work[:, 0:NIP]

        DREL = tables[:, 0:NIP]
        WT = tables[:, NIP:2 * NIP]
        SRCI = tables[:, 2 * NIP:3 * NIP].bitcast(I32)
        SB = tables[:, 3 * NIP:4 * NIP]
        OUT_OF = tables[:, 4 * NIP:5 * NIP]
        CS = tables[:, 5 * NIP:6 * NIP]
        fw1s = tables[:, 0:KC * H].rearrange("p (c h) -> p c h", c=KC)
        fw2s = tables[:, KC * H:KC * H + HC * D].rearrange("p (c d) -> p c d", c=HC)
        ROW_D, ROW_SA, ROW_SB = range(3)

        def carve(start, *sizes):
            views, at = [], start
            for n in sizes:
                views.append(work[:, at:at + n])
                at += n
            assert at <= WORK
            return views
        DSTR, SRCR, DSTF, HIB, CMPD, CMPS, PADM, PADR = carve(0, EC + 2, EC, EC + 2, EC, EC // 2, EC // 2, W, 3 * P)
        DSTR, SRCR, PADR = DSTR.bitcast(I32), SRCR.bitcast(I32), PADR.bitcast(I32)
        HID, HIS = (a_.bitcast(BF16) for a_ in (HIB[:, 0:EC // 2], HIB[:, EC // 2:EC]))
        CMPD, CMPS = CMPD.bitcast(BF16), CMPS.bitcast(BF16)
        G, OH, OHT = carve(0, U * W, 4 * P, 2 * P)
        G = G.rearrange("p (u w) -> p u w", w=W)
        OH = OH.rearrange("p (s n) -> p s n", s=4)
        OHT = OHT.rearrange("p (s n) -> p s n", s=2)
        XR, XT, ZB = carve(0, 2 * CH * D, 2 * D, 2 * D)
        XR = XR.rearrange("p (s t d) -> p s t d", s=2, d=D)
        XT = XT.rearrange("p (s c n) -> p s c n", s=2, c=KC)
        ZB = ZB.rearrange("p (s d) -> p s d", s=2)
        TE = T * NE
        LG, PR, EQ, OHB, TOT, INC, TI = carve(0, TE, TE, TE, 2 * TE, 2 * TE, 2 * TE, 4 * T)
        A_OH = work[:, 0:4 * P]
        B_OH, C_OH = work[:, 3 * TE:3 * TE + 8 * NT], work[:, 3 * TE + 8 * NT:3 * TE + 12 * NT]
        assert 4 * P <= 2 * TE and 12 * NT <= 4 * TE
        C_OH = C_OH.rearrange("p (s n) -> p s n", s=4)
        A_OH = A_OH.rearrange("p (s n) -> p s n", s=4)
        B_OH = B_OH.rearrange("p (s n) -> p s n", s=4)
        IDT = INC[:, TE:TE + T]
        GT = INC[:, TE + T:TE + 3 * T].rearrange("p (s t) -> p s t", s=2)
        PR3, EQ3, LG3 = (a_.rearrange("p (t e) -> p t e", e=NE) for a_ in (PR, EQ, LG))
        OH1, OH2 = (OHB[:, k * TE:(k + 1) * TE].rearrange("p (t e) -> p t e", e=NE) for k in range(2))
        EXC, PA = TOT[:, 0:TE], TOT[:, TE:2 * TE].rearrange("p (t e) -> p t e", e=NE)
        HILO = TI[:, 0:4 * T].rearrange("p (h s t) -> p h s t", h=2, s=2)
        TII = EQ[:, 0:4 * T].bitcast(I32).rearrange("p (h s t) -> p h s t", h=2, s=2)
        HS, HTS, GX, XE, YO, NIDX = carve(0, H, H, 2 * D, 2 * D, 2 * D, 4)
        HTS = HTS.rearrange("p (c n) -> p c n", c=HC)
        GX = GX.rearrange("p (s d) -> p s d", s=2)
        XE = XE.rearrange("p (s c n) -> p s c n", s=2, c=KC)
        YO = YO.rearrange("p (s d) -> p s d", s=2)
        GIDX, SIDX = NIDX[:, 0:2].bitcast(I32), NIDX[:, 2:4].bitcast(I32)

        tb = reg_b[:, T * (D + 1):]
        SOH = tb[:, 0:8 * P].rearrange("p (s n) -> p s n", s=8)
        gws = tb[:, 0:2 * KC * D].rearrange("p (l c d) -> p l c d", l=2, c=KC)
        GB1B, GB2B, GAMB, BETB, FB2B, FWRB = (tb[:, 2 * KC * D + k * D:2 * KC * D + (k + 1) * D] for k in range(6))
        FBR = BRB[:, NE:NE + 1]
        gate_t, gidx_t, sidx_t = (slot_t[:, k * (NT + 2):(k + 1) * (NT + 2)] for k in range(3))
        gidx_t, sidx_t = gidx_t.bitcast(I32), sidx_t.bitcast(I32)
        taken = [0]

        def sm(n):
            taken[0] += n
            return small[:, taken[0] - n:taken[0]]
        BOH = sm(4 * 26).bitcast(BF16).rearrange("p (s n) -> p s n", s=4)
        STG, PIDX = sm(U).bitcast(I32), sm(U).bitcast(I32)
        POS, JUNK = sm(4), sm(64)
        CNT = sm(104)
        ZERO = sm(2 * NT)
        MV = sm(4 * T).rearrange("p (s t k) -> p s t k", s=2, k=2)
        MV6 = sm(2 * 6 * CH).rearrange("p (s t k) -> p s t k", s=2, k=6)
        SQ, RS, NB = (sm(2 * T).rearrange("p (s t) -> p s t", s=2) for _ in range(3))
        DO, DI, T1 = sm(T), sm(T), sm(T)
        EPSC, ZEROC, PCOL = sm(1), sm(1), sm(1)
        SGN = sm(T - 1)
        J7 = sm(NIT)
        ST, STI, BLF, ENF, NB49, INCL, OFF, KK, DK, TJ = (sm(T + 1) for _ in range(10))
        STS = sm(T + 1)
        BSEL, KSL, ATB, ATK, ATC = (sm(NIT) for _ in range(5))
        BLKI = sm(NIT).bitcast(I32)
        STI = STI.bitcast(I32)
        VAL = sm(T)
        WV = sm(T)
        RM, PK = sm(T), sm(2 * T).rearrange("p (s t) -> p s t", s=2)
        DESC, TOFF, TLN, PB = (sm(NE) for _ in range(4))
        TLI = sm(NE).bitcast(I32)
        SC = sm(24)
        CNTS = sm(7)
        EDGE = sm(3).bitcast(I32)
        EF, EI = sm(2), sm(2).bitcast(I32)
        DISORDER = sm(1).bitcast(I32)
        assert taken[0] <= SMALL, taken[0]

        ps = [ctx.enter_context(nc.psum_tensor(f"bank{k}", [P, 512], F32)) for k in range(8)]
        sems = {}

        def z(name):
            if name not in sems:
                sems[name] = ctx.enter_context(nc.semaphore(name))
            return sems[name]

        def nodes(a, c, n=CH):
            return a[c * CH * P:(c * CH + n) * P, :].rearrange("(t p) d -> p t d", p=P)

        def row1(a, n):
            return a.rearrange("(a n) -> a n", a=1).to_broadcast([P, n])

        def load_offsets(engine, row, i, most, n=4):
            return nc.values_load_multi_w_load_instructions(
                rows[0:1, row, bass.ds(i, n)], engines=[engine], min_val=0, max_val=most,
                skip_runtime_bounds_check_because=IN_RANGE)[1]

        POOL_ = mybir.EngineType.Pool
        PE_, DVE_, SP_, ACT_ = (mybir.EngineType.PE, mybir.EngineType.DVE, mybir.EngineType.SP,
                                mybir.EngineType.Activation)
        block = ctx.enter_context(nc.Block())

        NORMS = dict(ln0=("a", 0), ln1=("a", 1), ln3=("a", 2), ln5=("a", 3), ln2=("b", 0), ln4=("b", 1))

        def norms(tag, what, c=0):
            which, before = NORMS[tag]
            return z(f"norm_{what}_{which}"), c + before * NCH

        def disorder(engine):
            return nc.values_load_multi_w_load_instructions(
                DISORDER[0:1, 0:1], engines=[engine], min_val=0, max_val=E,
                skip_runtime_bounds_check_because=IN_RANGE)[1][0]

        def rows_out(k, before, n=None):
            each = (NCH + 1 - k) // 2
            return z(f"rows_out{k}"), 16 * (before * each + (each if n is None else n))

        assert EC % 2 == 0
        B_ACT = 5
        CONST = 7
        ACC_CUT = 20 * (D + 1)
        PAR_IN = 8 * 16
        NFT = NF + NF % 2
        assert NFT * P <= N
        SEARCH = [(28, 3), (25, 3), (22, 3), (19, 3), (16, 3), (13, 3), (10, 3), (7, 3), (4, 3), (1, 3), (0, 1)]
        MOE = dict(tag="moe", tiles=NT, tiles_before=0, bias=4 * NE, gelu=ACT.Gelu, table=xn2_t, target=x2_t)
        FFN = dict(tag="ffn", tiles=NFT, tiles_before=NT, bias=4 * NE + NE * HC, gelu=ACT.Gelu_apprx_tanh, table=xn4_t, target=out)

        TILES_BEFORE = dict(rt=0, c1=T, c2=2 * T)
        BEFORE = dict(p1=NI, p2=2 * NI)

        def expert(engine, j):
            return nc.values_load_multi_w_load_instructions(
                etab[0:1, bass.ds(j, 1)], engines=[engine], min_val=0, max_val=NE - 1,
                skip_runtime_bounds_check_because=IN_RANGE)[1][0]

        def per_node(a_, n=NE):
            return a_.rearrange("p (t o) -> p t o", o=1).to_broadcast([P, a_.shape[1], n])

        def per_column(a_, n):
            return a_.rearrange("p (o d) -> p o d", o=1).to_broadcast([P, n, a_.shape[1]])

        REL = JUNK[:, 0:U]

        def message_loads(eng, which, half):
            for u in range(U):
                eng.wait_ge(z(f"ring_dma{u}"), 16 * ROUNDS)
            eng.wait_ge(z("msg_pad"), 32)

            def body(i0, first):
                v = load_offsets(which, ROW_SB, i0, NBLK - 1, U)
                for u in range(2 * half, U, 4):
                    if not first:
                        eng.wait_ge(z("s_mm"), i0 + u + 2 - U)
                    eng.dma_start(G[:, u:u + 2, :],
                                  msgs[bass.ds(v[u] * P, 2 * P), :].rearrange("(p s) w -> p s w", s=2)
                                  ).then_inc(z(f"sorted_in{u // 2}"), 16)
            eng.wait_ge(z("rows_set"), 5)
            body(0, True)
            with eng.Fori(U, NIS, U) as i0:
                body(i0, False)

        @block.sync
        def _(sp):
            sp.dma_start(DSTR[0:EP, 0:EC], dst.rearrange("(p j) -> p j", p=EP)).then_inc(z("edges_in"), 16)
            sp.dma_start(SRCR[0:EP, 0:EC], src.rearrange("(p j) -> p j", p=EP)).then_inc(z("edges_in"), 16)
            sp.wait_ge(z("pads_set"), 1)
            sp.dma_start(DSTR[0:EP - 1, EC:EC + 1],
                         dst[EC:E].rearrange("(p j) -> p j", p=EP - 1)[:, 0:1],
                         allow_slow_non_contiguous=True).then_inc(z("edges_in"), 16)
            for c in range(NCH):
                n = CH - (c == NCH - 1)
                sp.dma_start(X[:, c * CH:c * CH + n, :], nodes(x, c, n)).then_inc(z(f"x_in{c}"), 16)
            sp.dma_start(X[0:LAST, T - 1, :], x[(T - 1) * P:N, :]).then_inc(z(f"x_in{NCH - 1}"), 16)
            full = (NBLK - 1) * P
            for a, arr in enumerate((dst, src, edge_weight.bitcast(I32))):
                sp.dma_start(rec[0:NBLK - 1, a, :], arr[0:full].rearrange("(b j) -> b j", j=P)).then_inc(z("rec_in"), 16)
                sp.dma_start(rec[NBLK - 1:NBLK, a, 0:TAIL],
                             arr[full:E].rearrange("(b j) -> b j", b=1)).then_inc(z("rec_in"), 16)
                sp.dma_start(rec[NBLK - 1:NBLK, a, TAIL:P],
                             PADR[0:1, a * P:a * P + P - TAIL]).then_inc(z("rec_in"), 16)
            sp.dma_start(msgs[E:NBLK * P, :], PADM[0:NBLK * P - E, :]).then_inc(z("msg_pad"), 16)
            sp.dma_start(msgs[NBLK * P:(NBLK + 1) * P, :], PADM[:, :]).then_inc(z("msg_pad"), 16)
            r = 0
            for a in (ln_g.rearrange("e (c p) -> (e c) p", p=P), ln_b.rearrange("e (c p) -> (e c) p", p=P),
                      b1.rearrange("e (c p) -> (e c) p", p=P), fb1.rearrange("(c p) -> c p", p=P)):
                sp.dma_start(PT[r:r + a.shape[0], :], a).then_inc(z("par_in"), 16)
                r += a.shape[0]
            sp.dma_start(WRS[:, :, :], Wr.rearrange("(c p) e -> p c e", p=P)).then_inc(z("par_in"), 16)
            sp.dma_start(B2B[:], row1(b2.rearrange("e d -> (e d)"), NE * D)).then_inc(z("par_in"), 16)
            sp.dma_start(BRB[:, 0:NE], row1(br, NE)).then_inc(z("par_in"), 16)
            sp.dma_start(FBR, row1(fbr, 1)).then_inc(z("par_in"), 16)

            message_loads(sp, SP_, 0)


            for c in range(NCH + 3):
                if c < NCH:
                    sp.wait_ge(z("x1_set"), c + 1)
                    sp.dma_start(nodes(x2_t, c), X[:, c * CH:(c + 1) * CH, :]).then_inc(z("x1_out"), 16)
                if c >= 3:
                    sp.wait_ge(*norms("ln2", "norm", c - 2))
                    sp.dma_start(nodes(xn2_t, c - 3), XR[:, (c - 3) % 2, :, :]).then_inc(z(f"rows_out{(c - 3) % 2}"), 16)
            sp.dma_start(x2_t[T * P:FPAD, :], X[:, 0, :]).then_inc(z("x1_out"), 16)
            sp.wait_ge(z("x1_out"), 16 * (NCH + 1))
            sp.wait_ge(*norms("ln1", "norm", NCH))
            for e in range(NE):
                sp.dma_start(w1s[:, e, :, :], W1[e].rearrange("(c p) h -> p c h", p=P)).then_inc(z("w1_in"), 16)
            sp.wait_ge(z("tile_mm"), T)
            sp.wait_ge(*norms("ln2", "norm", NCH))
            for e in range(NE):
                sp.dma_start(w2s[:, e, :, :], W2[e].rearrange("(c p) d -> p c d", p=P)).then_inc(z("w2_in"), 16)
            for k in range(2):
                sp.wait_ge(z(f"net_added{k}"), 16 * (NT // 2))
            for c in range(NCH):
                sp.dma_start(X[:, c * CH:(c + 1) * CH, :], nodes(x2_t, c)).then_inc(z(f"x_in{c}"), 16)
            for l, a in enumerate((gW1, gW2)):
                sp.dma_start(gws[:, l, :, :], a.rearrange("(c p) d -> p c d", p=P)).then_inc(z("tail_in"), 16)
            for to, a in ((GB1B, gb1), (GB2B, gb2), (GAMB, gamma), (BETB, beta), (FB2B, fb2)):
                sp.dma_start(to, row1(a, D)).then_inc(z("tail_in"), 16)
            sp.dma_start(FWRB, row1(fwr.rearrange("d o -> (d o)"), D)).then_inc(z("tail_in"), 16)
            for c in range(NCH):
                sp.wait_ge(*norms("ln3", "norm", c + 1))
                sp.dma_start(nodes(conv1_t, c), XR[:, c % 2, :, :]).then_inc(z(f"rows_out{c % 2}"), 16)
            for c in range(NCH):
                sp.wait_ge(z("relu1"), (c + 1) * CH)
                sp.dma_start(nodes(conv2_t, c), XR[:, c % 2, :, :]).then_inc(z(f"rows_out{c % 2}"), 16)
            sp.wait_ge(z("p2_add"), NI + 1)
            sp.wait_ge(z("p2_stg"), NI)
            sp.dma_start(fw1s[:, :, :], fw1.rearrange("(c p) h -> p c h", p=P)).then_inc(z("fw_in"), 16)
            sp.dma_start(fw2s[:, :, :], fw2.rearrange("(c p) d -> p c d", p=P)).then_inc(z("fw_in"), 16)
            for c in range(NCH):
                n = CH - (c == NCH - 1)
                sp.wait_ge(*norms("ln4", "norm", c + 1))
                sp.dma_start(nodes(xn4_t, c), ACC[:, c * CH:(c + 1) * CH, 0:D]).then_inc(z("xn4_out"), 16)
                sp.wait_ge(z("sum_set"), c + 1)
                sp.dma_start(nodes(out, c, n), X[:, c * CH:c * CH + n, :]).then_inc(z("sum_out"), 16)
            sp.dma_start(out[(T - 1) * P:N, :], X[0:LAST, T - 1, :]).then_inc(z("sum_out"), 16)
            sp.wait_ge(z("xn4_out"), 16 * NCH)
            sp.wait_ge(z("sum_out"), 16 * (NCH + 1))
            sp.wait_ge(z("par_in"), PAR_IN)
            for k in range(2):
                sp.wait_ge(z(f"net_added{k}"), 16 * ((NT + NFT) // 2))

        @block.gpsimd
        def _(pool):
            g = nc.gpsimd
            ok = dict(allow_small_or_imprecise_dtypes=True)
            g.iota(IOTA[:], [[1, P]], base=0, channel_multiplier=0, **ok).then_inc(z("const"), 1)
            g.iota(J7, [[P, NIT]], base=0, channel_multiplier=1, **ok).then_inc(z("const"), 1)
            g.iota(PCOL, [[0, 1]], base=0, channel_multiplier=1, **ok).then_inc(z("const"), 1)
            g.memset(ONES[:], 1.0).then_inc(z("const"), 1)
            g.memset(IDENT[:], 0.0).then_inc(z("const"), 1)
            pool.wait_ge(z("const"), 5)
            g.affine_select(out=IDENT[:], in_=IDENT[:], compare_op=ALU.not_equal, fill=1.0, base=0,
                            pattern=[[1, P]], channel_multiplier=-1).then_inc(z("const"), 1)
            g.affine_select(out=TRI[:], in_=ONES[:], compare_op=ALU.is_gt, fill=0.0, base=0,
                            pattern=[[1, P]], channel_multiplier=-1).then_inc(z("const"), 1)
            pool.wait_ge(z("rec_in"), 9 * 16)
            pool.wait_ge(z("disorder_set"), 1)
            with pool.If(disorder(POOL_) > 0):
                pool.dma_start(raw.rearrange("b a j -> b (a j)"), rec.rearrange("b a j -> b (a j)")
                               ).then_inc(z("fix_in"), 16)
                pool.wait_ge(z("fix_in"), 16)
                with pool.Fori(0, NBLK) as b_:
                    pool.dma_start(EDGE[:, :], raw[bass.ds(b_, 1), :, :].rearrange("b a j -> j (b a)"),
                                   allow_slow_non_contiguous=True).then_inc(z("fix_in"), 16)
                    pool.wait_ge(z("fix_idx"), b_ + 1)
                    pool.sem_inc(z("turn"), 1)
                    for a_ in range(3):
                        pool.wait_ge(z("const"), CONST)
                        g.indirect_dma_start(rec.rearrange("b a (j o) -> (b a j) o", o=1),
                                             bass.IndirectOffsetOnAxis(ap=EI[:, 1:2], axis=0),
                                             EDGE[:, a_:a_ + 1], None, element_offset=a_ * P,
                                             bounds_check=(NBLK - 1) * 3 * P + P - 1, oob_is_err=False
                                             ).then_inc(z("fix_in"), 16)
                    pool.wait_ge(z("fix_in"), b_ * 64 + 80)
            pool.wait_ge(z("blocks_set"), 1)
            for k in range(NIT):
                g.indirect_dma_start(recs[:, k, :, :].rearrange("p a j -> p (a j)"), None,
                                     rec.rearrange("b a j -> b (a j)"),
                                     bass.IndirectOffsetOnAxis(ap=BLKI[:, k:k + 1], axis=0)
                                     ).then_inc(z("rec_out"), 16)

            pool.wait_ge(z("msg_pad"), 32)
            with pool.Fori(0, NI, U) as i0:
                for u in range(U):
                    pool.wait_ge(z("m_row"), i0 + u + 1)
                    pool.wait_ge(z("m_idx"), i0 + u + 1)
                    pool.sem_inc(z("turn"), 1)
                    pool.wait_ge(z("const"), CONST)
                    g.indirect_dma_start(msgs, bass.IndirectOffsetOnAxis(ap=PIDX[:, u:u + 1], axis=0),
                                         G[:, u, :], None, bounds_check=E - 1, oob_is_err=False
                                         ).then_inc(z(f"ring_dma{u}"), 16)
            pool.wait_ge(z("m_mm"), NI)
            g.memset(ACCf[:, ACC_CUT:], 0.0).then_inc(z("acc_zero"), 1)


            def network(tag, tiles, tiles_before, table, target, **_):
                def gather(j, s, dynamic=True):
                    pool.wait_ge(z("net_gidx"), j + 1 + tiles_before)
                    if dynamic:
                        pool.wait_ge(z("net_tr"), j - 1 + tiles_before)
                        pool.sem_inc(z("turn"), 1)
                    pool.wait_ge(z("const"), CONST)
                    g.indirect_dma_start(GX[:, s, :], None, table,
                                         bass.IndirectOffsetOnAxis(ap=GIDX[:, s:s + 1], axis=0)
                                         ).then_inc(z(f"net_in{s}"), 16)

                def scatter(j, s, last):
                    pool.wait_ge(z("net_out"), j + 1 + tiles_before)
                    if last is not None:
                        pool.wait_ge(z(f"net_added{1 - s}"), last + tiles_before * 8)
                    pool.sem_inc(z("turn"), 1)
                    pool.wait_ge(z("const"), CONST)
                    g.indirect_dma_start(target, bass.IndirectOffsetOnAxis(ap=SIDX[:, s:s + 1], axis=0),
                                         YO[:, s, :], None, compute_op=ALU.add).then_inc(z(f"net_added{s}"), 16)
                gather(0, 0, False)
                gather(1, 1, False)
                gather(2, 0)
                gather(3, 1)
                scatter(0, 0, None)
                with pool.Fori(1, tiles - 4, 2) as j0:
                    gather(j0 + 3, 0)
                    scatter(j0, 1, j0 * 8 + 8)
                    gather(j0 + 4, 1)
                    scatter(j0 + 1, 0, j0 * 8 + 8)
                scatter(tiles - 3, 1, (tiles - 2) * 8)
                scatter(tiles - 2, 0, (tiles - 2) * 8)
                scatter(tiles - 1, 1, tiles * 8)

            def gathers(tag, table):
                def body(i0, first):
                    for u in range(U):
                        if u % 8 == 0:
                            pool.wait_ge(z(f"{tag}_stg"), i0 + u + 8)
                        if not first:
                            pool.wait_ge(z(f"{tag}_mm"), i0 + u + 1 - U)
                        if u % 8 == 0 or not first:
                            pool.sem_inc(z("turn"), 1)
                        pool.wait_ge(z("const"), CONST)
                        g.indirect_dma_start(G[:, u, 0:D], None, table,
                                             bass.IndirectOffsetOnAxis(ap=STG[:, u:u + 1], axis=0)
                                             ).then_inc(z(f"ring_dma{u}"), 16)
                body(0, True)
                with pool.Fori(U, NI, U) as i0:
                    body(i0, False)

            def chunk(c):
                w_ = slice(c * CH, (c + 1) * CH)
                return X[:, w_, :], ACC[:, w_, 0:D]

            pool.wait_ge(z("s_add"), NIS + 1)
            for c in range(NCH):
                x_, sums = chunk(c)
                g.tensor_tensor(x_, x_, sums, ALU.add).then_inc(z("x1_set"), 1)
            pool.wait_ge(z("x1_out"), 16 * (NCH + 1))
            for k in range(2):
                pool.wait_ge(*rows_out(k, 0))
            network(**MOE)
            for k in range(2):
                pool.wait_ge(z(f"net_added{k}"), 16 * (NT // 2))
            pool.wait_ge(z("net_mm2"), NT)
            g.memset(ACCf, 0.0).then_inc(z("acc1_zero"), 1)
            for k in range(2):
                pool.wait_ge(*rows_out(k, 1))
            gathers("p1", conv1_t)
            pool.wait_ge(z("tail_in"), 8 * 16)
            pool.wait_ge(*norms("ln3", "norm", NCH))
            g.tensor_tensor(X, X, per_column(BETB, T), ALU.add).then_inc(z("beta_in"), 1)
            for k in range(2):
                pool.wait_ge(*rows_out(k, 2))
            gathers("p2", conv2_t)
            pool.wait_ge(z("beta_in"), 1)
            for c in range(NCH):
                x_, h = chunk(c)
                pool.wait_ge(*norms("ln5", "norm", c + 1))
                g.tensor_tensor(h, h, per_column(GAMB, CH), ALU.mult).then_inc(z("scaled"), 1)
                pool.wait_ge(z("scaled"), c + 1)
                g.tensor_tensor(x_, x_, h, ALU.add).then_inc(z("x3_set"), 1)
            for c in range(NCH):
                x_, h = chunk(c)
                pool.wait_ge(*norms("ln4", "norm", c + 1))
                g.tensor_tensor(x_, x_, h, ALU.add).then_inc(z("sum_set"), 1)
            pool.wait_ge(z("xn4_out"), 16 * NCH)
            pool.wait_ge(z("sum_out"), 16 * (NCH + 1))
            network(**FFN)

        @block.scalar
        def _(act):
            a = nc.scalar
            astep = Chain(act, z("a_step"))

            def ln_std(tag, c, s=0):
                act.wait_ge(*norms(tag, "var", c + 1))
                a.activation(SQ[:, s, c * CH:(c + 1) * CH], MV[:, s, c * CH:(c + 1) * CH, 1], ACT.Sqrt,
                             bias=EPSC).then_inc(norms(tag, "std")[0], 1)

            def ln_apply(tag, c, src, dst_, s=0, between=None):
                act.wait_ge(*norms(tag, "scale", c + 1))
                for i in range(CH):
                    t = c * CH + i
                    ins = a.activation(dst_(i), src(i), ACT.Identity, bias=NB[:, s, t:t + 1], scale=RS[:, s, t:t + 1])
                    if between is not None:
                        between(t)
                ins.then_inc(norms(tag, "norm")[0], 1)

            for c in range(NCH + 1):
                if c < NCH:
                    ln_std("ln0", c)
                if c >= 1:
                    ln_apply("ln0", c - 1, lambda i: X[:, (c - 1) * CH + i, :], lambda i: XN[:, (c - 1) * CH + i, :])
            act.wait_ge(z("edges_f"), 1)
            act.wait_ge(z("small_set"), 1)
            for b in range(B_ACT, T):
                astep(a.activation(CMPS[0:EP, :], HIS[0:EP, :], ACT.Sign, bias=SGN[0:EP, b - 1:b], scale=-1.0,
                                   accum_out=CNT[0:EP, 52 + b:53 + b]))

            def onehot_t(i, j, wait_free):
                act.wait_ge(z("m_tr"), i + 1)
                if wait_free:
                    act.wait_ge(z("m_mm"), i - 1)
                a.copy(OHT[:, j % 2, :], ps[j % 2][:, 0:P]).then_inc(z("m_oht"), 1)
            onehot_t(0, 0, False)

            def message_body(i0, first):
                for u in range(U):
                    i = i0 + u
                    onehot_t(i + 1, u + 1, not (first and u < 1))
                    act.wait_ge(z("m_mm"), i + 1)
                    if not first:
                        act.wait_ge(z(f"ring_dma{u}"), i0)
                    a.copy(G[:, u, 0:D], ps[3 + u % 2][:, 0:D]).then_inc(z("m_row"), 1)
            message_body(0, True)
            with act.Fori(U, NI, U) as i0:
                message_body(i0, False)
            message_loads(act, ACT_, 1)


            def inv_root(tag, y):
                act.wait_ge(z(f"{tag}_y"), 1)
                a.activation(SQ[:, 0, :], y, ACT.Sqrt).then_inc(z(f"{tag}_root"), 1)

            def scale_onehots(tag, tiles, steps, value):
                for n in range(steps):
                    s, t = n // T, n % T
                    act.wait_ge(z(f"{tag}_oh"), n + 1)
                    a.activation(B_OH[:, n % 4, 0:tiles], C_OH[:, n % 4, 0:tiles], ACT.Copy, scale=IDT[:, t:t + 1])
                    a.activation(B_OH[:, n % 4, tiles:2 * tiles], C_OH[:, n % 4, 0:tiles], ACT.Copy, scale=value(s, t)
                                 ).then_inc(z(f"{tag}_scaled"), 1)

            def network(tag, tiles, tiles_before, bias, gelu, **_):
                def hidden(j, e, first):
                    act.wait_ge(z("net_htr"), j + 1 + tiles_before)
                    if not first:
                        act.wait_ge(z("net_mm2"), j + tiles_before)
                    for k in range(HC):
                        col = bias + k if e is None else e * HC + (bias + k)
                        ins = a.activation(HTS[:, k, :], ps[3 + k // 4][:, k % 4 * P:(k % 4 + 1) * P], gelu,
                                           bias=PT[:, bass.ds(col, 1)])
                    ins.then_inc(z("net_gelu"), 1)

                def e_(j):
                    return expert(ACT_, j) if tag == "moe" else None
                act.wait_ge(z("slots"), 1 + (tag == "ffn"))
                hidden(0, e_(0), True)
                hidden(1, e_(1), False)
                with act.Fori(2, tiles, 2) as j0:
                    for s in range(2):
                        hidden(j0 + s, e_(j0 + s), False)

            def staging(tag):
                def body(i0, first):
                    for h in range(0, U, 8):
                        if not first:
                            for u in range(h, h + 8):
                                act.wait_ge(z(f"ring_dma{u}"), i0 + BEFORE[tag])
                        a.copy(STG[:, h:h + 8], SRCI[:, bass.ds(i0 + h, 8)]).then_inc(z(f"{tag}_stg"), 8)
                body(0, True)
                with act.Fori(U, NI, U) as i0:
                    body(i0, False)

            def evacuate(tag, t):
                act.wait_ge(z("tile_tr"), t + 1 + TILES_BEFORE[tag])
                if t >= 2:
                    act.wait_ge(z("tile_mm"), t - 1 + TILES_BEFORE[tag])
                a.copy(XT[:, t % 2, :, :].rearrange("p c n -> p (c n)"), ps[t % 2][:, 0:D]).then_inc(z("tile_xt"), 1)

            inv_root("do", DI)
            for c in range(NCH + 3):
                if c < NCH:
                    ln_std("ln1", c)
                if 1 <= c <= NCH:
                    ln_apply("ln1", c - 1, lambda i: X[:, (c - 1) * CH + i, :], lambda i: ACC[:, (c - 1) * CH + i, 0:D])
                if 2 <= c <= NCH + 1:
                    ln_std("ln2", c - 2, 1)
                if c >= 3:
                    if c >= 5:
                        act.wait_ge(*rows_out((c - 3) % 2, 0, (c - 3) // 2))
                    ln_apply("ln2", c - 3, lambda i: ACC[:, (c - 3) * CH + i, 0:D], lambda i: XR[:, (c - 3) % 2, i, :], 1,
                             lambda t: evacuate("rt", t))
            act.wait_ge(z("logits_set"), 1)
            a.activation(PR, LG, ACT.Exp).then_inc(z("exp_set"), 1)
            scale_onehots("moe", NT, 2 * T, lambda s, t: GT[:, s, t:t + 1])
            network(**MOE)
            for c in range(NCH + 1):
                if c < NCH:
                    ln_std("ln3", c)
                if c >= 1:
                    if c >= 3:
                        act.wait_ge(*rows_out((c - 1) % 2, 1, (c - 1) // 2))
                    ln_apply("ln3", c - 1, lambda i: X[:, (c - 1) * CH + i, :], lambda i: XR[:, (c - 1) % 2, i, :])
            staging("p1")
            inv_root("di", RM)
            evacuate("c1", 0)
            for t in range(T):
                if t + 1 < T:
                    evacuate("c1", t + 1)
                c = t // CH
                act.wait_ge(z("lin1"), t + 1)
                if c >= 2 and t % CH == 0:
                    act.wait_ge(*rows_out(c % 2, 2, c // 2))
                a.activation(XR[:, c % 2, t % CH, :], ZB[:, t % 2, :], ACT.Relu, scale=DO[:, t:t + 1]
                             ).then_inc(z("relu1"), 1)
            staging("p2")
            evacuate("c2", 0)
            for t in range(T):
                if t + 1 < T:
                    evacuate("c2", t + 1)
                c = t // CH - 1
                if c >= 0 and t % CH == 2:
                    ln_std("ln5", c)
                if c >= 0 and t % CH == 5:
                    ln_apply("ln5", c, *[lambda i: ACC[:, c * CH + i, 0:D]] * 2)
            c = NCH - 1
            ln_std("ln5", c)
            ln_apply("ln5", c, *[lambda i: ACC[:, c * CH + i, 0:D]] * 2)
            for c in range(NCH + 1):
                if c < NCH:
                    ln_std("ln4", c, 1)
                if c >= 1:
                    ln_apply("ln4", c - 1, lambda i: X[:, (c - 1) * CH + i, :], lambda i: ACC[:, (c - 1) * CH + i, 0:D], 1)
            scale_onehots("ffn", NFT, T, lambda s, t: WV[:, t:t + 1])
            network(**FFN)

        @block.vector
        def _(v):
            step = Chain(v, z("v_step"))

            def ln_stats(tag, c, src_, s=0):
                if c:
                    v.wait_ge(*norms(tag, "var", c))
                for i in range(CH):
                    ins = v.bn_stats(MV6[:, s, i, :], src_(i))
                step(ins)
                for i in range(CH):
                    ins = v.bn_aggr(MV[:, s, c * CH + i, :], MV6[:, s, i, :])
                ins.then_inc(norms(tag, "var")[0], 1)

            def newton(r, t, y, add):
                step(v.scalar_tensor_tensor(t, y, add, r, ALU.add, ALU.mult))
                step(v.tensor_tensor(t, t, r, ALU.mult))
                step(v.tensor_scalar(t, t, -0.5, 1.5, ALU.mult, ALU.add))
                step(v.tensor_tensor(r, r, t, ALU.mult))

            def ln_scale(tag, c, s=0, extra=None):
                w_ = slice(c * CH, (c + 1) * CH)
                r, n = RS[:, s, w_], NB[:, s, w_]
                v.wait_ge(*norms(tag, "std", c + 1))
                v.wait_ge(*norms(tag, "var", c + 1))
                step(v.reciprocal(r, SQ[:, s, w_]))
                newton(r, T1[:, 0:CH], MV[:, s, w_, 1], EPS)
                if extra is not None:
                    step(v.tensor_tensor(r, r, extra[:, w_], ALU.mult))
                v.scalar_tensor_tensor(n, MV[:, s, w_, 0], -1.0, r, ALU.mult, ALU.mult).then_inc(norms(tag, "scale")[0], 1)

            v.memset(X[96:P, T - 1, :], 0.0)
            v.memset(DSTR[0:P, EC:EC + 1], int(FAR))
            v.memset(PADM[:, 0:W - 1], 0.0)
            v.memset(PADM[:, W - 1:W], -FAR)
            v.memset(PADR[0:1, 0:P], -int(FAR))
            v.memset(PT[:], 0.0)
            step(v.memset(PADR[0:1, P:3 * P], 0))
            v.engine_nop().then_inc(z("pads_set"), 1)
            v.memset(EPSC, EPS)
            v.memset(etab[0:1, :], 0)
            v.memset(ZEROC, 0.0)
            v.memset(ZERO, 0.0)
            v.memset(CNT, 0.0)
            v.wait_ge(z("const"), 7)
            v.tensor_copy(TRIB[:, 0, :], TRI[:])
            v.tensor_scalar(TRIB[:, 1, :], TRI[:], -1.0, 1.0, ALU.mult, ALU.add)
            v.tensor_scalar(SGN, IOTA[:, 1:T], -0.5, None, ALU.add).then_inc(z("small_set"), 1)
            v.wait_ge(z("edges_in"), 48)
            step(v.tensor_scalar(SRCR[0:EP, :], SRCR[0:EP, :], 7, None, ALU.arith_shift_right))
            v.tensor_copy(HIS[0:EP, :], SRCR[0:EP, :]).then_inc(z("edges_f"), 1)
            step(v.tensor_copy(DSTF[0:EP, 0:EC + 1], DSTR[0:EP, 0:EC + 1]))
            step(v.tensor_scalar(DSTR[0:EP, 0:EC], DSTR[0:EP, 0:EC], 7, None, ALU.arith_shift_right))
            step(v.tensor_copy(HID[0:EP, :], DSTR[0:EP, 0:EC]))
            for c in range(NCH + 1):
                if c < NCH:
                    v.wait_ge(z(f"x_in{c}"), 16 * (1 + (c == NCH - 1)))
                    ln_stats("ln0", c, lambda i: X[:, c * CH + i, :])
                if c >= 1:
                    ln_scale("ln0", c - 1)
            for b in range(1, T):
                step(v.tensor_scalar(CMPD[0:EP, :], HID[0:EP, :], float(b), None, ALU.is_lt, ALU.add,
                                     accum_out=CNT[0:EP, b:b + 1]))
            step(v.scalar_tensor_tensor(CMPD[0:EP, :], DSTF[0:EP, 0:EC], 0.0, DSTF[0:EP, 1:EC + 1], ALU.add, ALU.is_gt,
                                        accum_out=CNT[0:EP, 50:51]))
            v.engine_nop().then_inc(z("counted_d"), 1)
            for b in range(1, B_ACT):
                step(v.tensor_scalar(CMPD[0:EP, :], HIS[0:EP, :], float(b), None, ALU.is_lt, ALU.add,
                                     accum_out=CNT[0:EP, 52 + b:53 + b]))
            v.engine_nop().then_inc(z("counted_s"), 1)

            def attributes(tot, source=False):
                st, hi, lo = ST[:, 0:T + 1], ST[:, 1:T + 1], ST[:, 0:T]
                step(v.tensor_copy(st, tot))
                if source:
                    h = ST[:, B_ACT:T]
                    step(v.tensor_scalar(h, h, 0.5, E / 2, ALU.mult, ALU.add))
                v.memset(ST[:, 0:1], 0.0)
                step(v.memset(ST[:, T:T + 1], float(E)))
                if source:
                    step(v.tensor_copy(STS[:, 0:T + 1], st))
                step(v.tensor_copy(STI[:, 0:T + 1], st))
                step(v.tensor_scalar(STI[:, 0:T + 1], STI[:, 0:T + 1], 7, None, ALU.arith_shift_right))
                step(v.tensor_copy(BLF[:, 0:T + 1], STI[:, 0:T + 1]))
                step(v.tensor_scalar(TJ[:, 0:T], hi, 1.0, None, ALU.subtract))
                step(v.tensor_copy(STI[:, 0:T], TJ[:, 0:T]))
                step(v.tensor_scalar(STI[:, 0:T], STI[:, 0:T], 7, None, ALU.arith_shift_right))
                step(v.tensor_copy(ENF[:, 0:T], STI[:, 0:T]))
                step(v.tensor_tensor(TJ[:, 0:T], hi, lo, ALU.is_gt))
                step(v.scalar_tensor_tensor(NB49[:, 0:T], ENF[:, 0:T], 1.0, BLF[:, 0:T], ALU.add, ALU.subtract))
                step(v.tensor_tensor(NB49[:, 0:T], NB49[:, 0:T], TJ[:, 0:T], ALU.mult))
                if source:
                    step(v.tensor_copy(STI[:, 0:T], NB49[:, 0:T]))
                    step(v.tensor_scalar(STI[:, 0:T], STI[:, 0:T], 1, None, ALU.bitwise_and))
                    step(v.tensor_copy(TJ[:, 0:T], STI[:, 0:T]))
                    step(v.tensor_tensor(NB49[:, 0:T], NB49[:, 0:T], TJ[:, 0:T], ALU.add))
                step(v.tensor_tensor_scan(INCL[:, 0:T], ONES[:, 0:T], NB49[:, 0:T], 0.0, ALU.mult, ALU.add))
                step(v.tensor_tensor(OFF[:, 0:T], INCL[:, 0:T], NB49[:, 0:T], ALU.subtract))
                step(v.tensor_tensor(KK[:, 0:T], BLF[:, 0:T], OFF[:, 0:T], ALU.subtract))
                step(v.tensor_tensor(DK[:, 0:T - 1], KK[:, 1:T], KK[:, 0:T - 1], ALU.subtract))
                for k in range(NIT):
                    v.tensor_scalar(JUNK[:, 0:T - 1], OFF[:, 1:T], J7[:, k:k + 1], None, ALU.is_le, ALU.add,
                                    accum_out=BSEL[:, k:k + 1])
                    step(v.scalar_tensor_tensor(TJ[:, 0:T - 1], OFF[:, 1:T], J7[:, k:k + 1], DK[:, 0:T - 1],
                                                ALU.is_le, ALU.mult, accum_out=KSL[:, k:k + 1]))
                step(v.tensor_copy(ATB, BSEL))
                step(v.tensor_tensor(ATK, KSL, J7, ALU.add))
                step(v.tensor_scalar(ATK, ATK, KK[:, 0:1], None, ALU.add))
                step(v.tensor_scalar(ATC, J7, INCL[:, T - 1:T], FAR, ALU.is_ge, ALU.mult))
                step(v.tensor_scalar(TJ[:, 0:NIT], ATK, float(NBLK), FAR, ALU.is_ge, ALU.mult))
                step(v.tensor_tensor(ATC, ATC, TJ[:, 0:NIT], ALU.max))
                step(v.tensor_scalar(ATK, ATK, float(NBLK - 1), None, ALU.min))
                step(v.scalar_tensor_tensor(ATC, ATB, float(P), ATC, ALU.mult, ALU.add))

            row_no = [0]

            def to_rows(attr):
                r = row_no[0]
                row_no[0] += 1
                v.tensor_tensor(DG, IDENT[:].rearrange("p (k n) -> p k n", k=1).to_broadcast([P, NIT, P]),
                                attr.rearrange("p (k n) -> p k n", n=1).to_broadcast([P, NIT, P]), ALU.mult
                                ).then_inc(z("diag_set"), 1)
                v.wait_ge(z("row_made"), r + 1)

            def row_out(ops, to):
                ops(to[:, 0:512], ps[1][0:to.shape[0], 0:512])
                ops(to[:, 512:NIP], ps[2][0:to.shape[0], 0:NIP - 512])

            v.wait_ge(z("totals_d"), 1)
            attributes(ps[0][:, 0:T + 1])
            step(v.tensor_copy(BLKI, ATK))
            v.engine_nop().then_inc(z("blocks_set"), 1)
            step(v.tensor_copy(DISORDER, ps[0][:, T + 1:T + 2]))
            v.engine_nop().then_inc(z("disorder_set"), 1)
            with v.If(disorder(DVE_) > 0):
                fix = Chain(v, z("fix_step"))
                with v.Fori(0, NBLK) as b_:
                    fix.enter(b_, 0, 9)
                    v.wait_ge(z("fix_in"), b_ * 64 + 32)
                    v.wait_ge(z("fix_rank"), b_ * 2 + 1)
                    fix(v.tensor_scalar(EI[:, 0:1], EDGE[:, 0:1], 7, None, ALU.arith_shift_right))
                    fix(v.tensor_copy(EF[:, 0:1], EI[:, 0:1]))
                    v.tensor_scalar(BOH[:, 0, 0:T], IOTA[:, 0:T], EF[:, 0:1], None, ALU.is_equal
                                    ).then_inc(z("fix_tile"), 1)
                    v.wait_ge(z("fix_rank"), b_ * 2 + 2)
                    fix(v.scalar_tensor_tensor(JUNK[:, 0:T], ps[5][:, 0:T], 1.0, BOH[:, 0, 0:T], ALU.mult, ALU.mult,
                                                accum_out=EF[:, 1:2]))
                    fix(v.tensor_scalar(EF[:, 0:1], EF[:, 0:1], 0.0, FAR, ALU.is_lt, ALU.mult))
                    fix(v.tensor_tensor(EF[:, 1:2], EF[:, 1:2], EF[:, 0:1], ALU.add))
                    fix(v.tensor_copy(EI[:, 0:1], EF[:, 1:2]))
                    fix(v.tensor_scalar(EI[:, 0:1], EI[:, 0:1], 7, None, ALU.arith_shift_right))
                    fix(v.tensor_copy(EF[:, 0:1], EI[:, 0:1]))
                    fix(v.scalar_tensor_tensor(EF[:, 1:2], EF[:, 0:1], float(2 * P), EF[:, 1:2], ALU.mult, ALU.add))
                    v.tensor_copy(EI[:, 1:2], EF[:, 1:2]).then_inc(z("fix_idx"), 1)
                fix.leave(NBLK)
            to_rows(ATB)
            row_out(lambda o_, i_: v.tensor_scalar(o_, i_, float(D), None, ALU.mult).then_inc(z("row_used"), 1),
                    rows[0:1, ROW_D, :])
            to_rows(ATC)
            row_out(lambda o_, i_: v.tensor_copy(o_, i_).then_inc(z("row_used"), 1), CD)
            v.wait_ge(z("totals_s"), 1)
            attributes(ps[0][:, 52:52 + T + 1], source=True)
            v.engine_nop().then_inc(z("starts_set"), 1)
            to_rows(ATB)
            row_out(lambda o_, i_: v.tensor_scalar(o_, i_, float(D + 1), None, ALU.mult).then_inc(z("row_used"), 1),
                    rows[0:1, ROW_SA, :])
            to_rows(ATK)
            row_out(lambda o_, i_: v.tensor_copy(o_, i_).then_inc(z("row_used"), 1), rows[0:1, ROW_SB, :])
            to_rows(ATC)
            row_out(lambda o_, i_: v.tensor_copy(o_, i_).then_inc(z("row_used"), 1), CS)
            v.wait_ge(z("row_used"), 10)
            v.engine_nop().then_inc(z("rows_set"), 5)
            for k in range(NIT):
                v.wait_ge(z("rec_out"), 16 * NIT)
                v.tensor_copy(RF[:, k, :, :], recs[:, k, 0:2, :]).then_inc(z("rec_f"), 1)
            for k in range(NIT):
                v.wait_ge(z("rec_t"), k + 1)
                c_ = slice(k * P, (k + 1) * P)
                pk = ps[3 + k % 2]
                v.tensor_tensor(DREL[:, c_], pk[:, 0:P], CD[:, c_], ALU.subtract)
                v.tensor_copy(SB[:, c_], pk[:, P:2 * P])
                v.tensor_copy(WT[:, c_], pk[:, 2 * P:3 * P]).then_inc(z("rec_used"), 1)
            v.wait_ge(z("rec_used"), NIT)
            step(v.tensor_scalar(OUT_OF, DREL, 0.0, None, ALU.is_ge))
            step(v.scalar_tensor_tensor(OUT_OF, DREL, float(P), OUT_OF, ALU.is_lt, ALU.mult))
            step(v.tensor_copy(SRCI, SB))
            HI = DG.rearrange("p k n -> p (k n)").bitcast(I32)
            step(v.tensor_scalar(HI, SRCI, 7, None, ALU.arith_shift_right))
            step(v.tensor_copy(SB, HI))
            step(v.scalar_tensor_tensor(SB, SB, 1.0, OUT_OF, ALU.add, ALU.mult))
            step(v.tensor_scalar(SB, SB, 1.0, None, ALU.subtract))
            step(v.tensor_scalar(OUT_OF, OUT_OF, -FAR, FAR, ALU.mult, ALU.add))

            v.wait_ge(z("msg_pad"), 32)
            v.wait_ge(z("rec_in"), 9 * 16)
            step(v.memset(G[:, :, D:D + 1], 1.0))

            def onehots(i, j, wait_free):
                if wait_free:
                    v.wait_ge(z("m_tr"), i - 3)
                v.tensor_scalar(OH[:, j % 4, :], IOTA[:], DREL[:, bass.ds(i, 1)], WT[:, bass.ds(i, 1)],
                                ALU.is_equal, ALU.mult).then_inc(z("m_oh"), 1)
                v.tensor_scalar(BOH[:, j % 4, 0:T], IOTA[:, 0:T], SB[:, bass.ds(i, 1)], None,
                                ALU.is_equal).then_inc(z("m_boh"), 1)
            onehots(0, 0, False)

            def message_body(i0, first):
                for u in range(U):
                    i = i0 + u
                    onehots(i + 1, u + 1, not (first and u < 3))
                    if u % 8 == 0:
                        if not first:
                            for w_ in range(u, u + 8):
                                v.wait_ge(z(f"ring_dma{w_}"), i0)
                        v.tensor_copy(G[:, u:u + 8, D + 1], SRCI[:, bass.ds(i, 8)]).then_inc(z("m_src"), 8)
                    v.wait_ge(z("m_rank"), i + 1)
                    v.scalar_tensor_tensor(JUNK[:, 0:T], ps[2][:, 0:T], 1.0, BOH[:, u % 4, 0:T], ALU.mult, ALU.mult,
                                           accum_out=POS[:, u % 4:u % 4 + 1]).then_inc(z("m_pos"), 1)
                    v.wait_ge(z("m_pos"), i + 1)
                    if u % 8 == 0:
                        v.wait_ge(z("m_src"), i + 8)
                    v.tensor_scalar(PIDX[:, u:u + 1], POS[:, u % 4:u % 4 + 1], OUT_OF[:, bass.ds(i, 1)], None,
                                    ALU.add).then_inc(z("m_idx"), 1)
            message_body(0, True)
            with v.Fori(U, NI, U) as i0:
                message_body(i0, False)

            v.wait_ge(z("m_mm"), NI)
            v.memset(ACCf[:, 0:ACC_CUT], 0.0).then_inc(z("acc_zero"), 1)
            v.wait_ge(z("acc_zero"), 2)

            v.engine_nop().then_inc(z("s_add"), 1)

            def s_onehots(i0, u):
                w_ = u % U
                v.wait_ge(z(f"sorted_in{w_ // 2}"), i0 + (16 if u < U else 32))
                rel = REL[:, w_:w_ + 2]
                v.tensor_tensor(rel, G[:, w_:w_ + 2, D + 1], CS[:, bass.ds(i0 + u, 2)], ALU.subtract
                                ).then_inc(z("s_rel"), 2)
                v.wait_ge(z("s_rel"), i0 + u + 2)
                v.tensor_tensor(SOH[:, u % 8:u % 8 + 2, :], IOTA[:].rearrange("p (o n) -> p o n", o=1).to_broadcast([P, 2, P]),
                                rel.rearrange("p (s o) -> p s o", o=1).to_broadcast([P, 2, P]),
                                ALU.is_equal).then_inc(z("s_oh"), 2)
            s_onehots(0, 0)
            s_onehots(0, 2)
            v.engine_nop().then_inc(z("s_add"), 1)

            def sum_body(i0, last):
                for u in range(0, U, 2):
                    i = i0 + u
                    if u % 8 == 0:
                        offs = load_offsets(DVE_, ROW_SA, i, (T - 1) * (D + 1), 8)
                    if not (last and u + 4 >= U):
                        s_onehots(i0, u + 4)
                    v.wait_ge(z("s_add"), i + 1)
                    v.wait_ge(z("s_mm"), i + 2)
                    acc = ACCf[:, bass.ds(offs[u % 8], D + 1)]
                    v.tensor_tensor(acc, acc, ps[u // 2 % 4][:, 0:D + 1], ALU.add).then_inc(z("s_add"), 2)
            with v.Fori(0, NIS - U, U) as i0:
                sum_body(i0, False)
            sum_body(NIS - U, True)


            def inv_root(tag, r, y):
                v.engine_nop().then_inc(z(f"{tag}_y"), 1)
                v.wait_ge(z(f"{tag}_root"), 1)
                step(v.reciprocal(r, SQ[:, 0, :]))
                newton(r, T1, y, 0.0)

            def invert(tag, tiles, steps):
                for n in range(steps):
                    s, t = n // T, n % T
                    if n >= 4:
                        v.wait_ge(z(f"{tag}_inv"), n - 2)
                    v.tensor_scalar(A_OH[:, n % 4, :], IOTA[:], HILO[:, 1, s, t:t + 1], None, ALU.is_equal)
                    v.tensor_scalar(C_OH[:, n % 4, 0:tiles], IOTA[:, 0:tiles], HILO[:, 0, s, t:t + 1], None,
                                    ALU.is_equal).then_inc(z(f"{tag}_oh"), 1)
                v.wait_ge(z(f"{tag}_inv"), steps + 1)
                r, free = A_OH.rearrange("p s n -> p (s n)")[:, 0:tiles], B_OH.rearrange("p s n -> p (s n)")[:, 0:tiles]
                step(v.tensor_scalar(r, ps[2][:, 0:tiles], 1.0, 0.0, ALU.subtract, ALU.max))
                step(v.tensor_copy(gidx_t[:, 0:tiles], r))
                step(v.tensor_scalar(free, ps[2][:, 0:tiles], 0.0, SC[:, 0:1], ALU.is_equal, ALU.mult))
                step(v.scalar_tensor_tensor(r, ps[2][:, 0:tiles], -1.0, free, ALU.add, ALU.add))
                step(v.tensor_copy(sidx_t[:, 0:tiles], r))
                step(v.tensor_copy(gate_t[:, 0:tiles], ps[2][:, tiles:2 * tiles]))
                v.engine_nop().then_inc(z("slots"), 1)

            def places(pos, n):
                step(v.tensor_copy(TII[:, 0, 0:n, :], pos[:, 0:n, :]))
                step(v.tensor_scalar(TII[:, 1, 0:n, :], TII[:, 0, 0:n, :], P - 1, None, ALU.bitwise_and))
                step(v.tensor_scalar(TII[:, 0, 0:n, :], TII[:, 0, 0:n, :], 7, None, ALU.arith_shift_right))
                step(v.tensor_copy(HILO[:, :, 0:n, :], TII[:, :, 0:n, :]))

            def network(tag, tiles, tiles_before, **_):
                experts = tag == "moe"

                def e_(j):
                    return expert(DVE_, j) if experts else None

                def stage_in(j, s, h0, first):
                    if not first:
                        v.wait_ge(z(f"net_in{s}"), h0 + tiles_before * 8)
                    v.tensor_copy(GIDX[:, s:s + 1], gidx_t[:, bass.ds(j, 1)]).then_inc(z("net_gidx"), 1)

                def normed(j, s, e):
                    v.wait_ge(z("net_tr"), j + 1 + tiles_before)
                    for c in range(KC):
                        i_ = ps[0][:, c * P:(c + 1) * P]
                        if experts:
                            ins = v.tensor_scalar(XE[:, s, c, :], i_, PT[:, bass.ds(e * KC + c, 1)],
                                                  PT[:, bass.ds(e * KC + (NE * KC + c), 1)], ALU.mult, ALU.add)
                        else:
                            ins = v.tensor_copy(XE[:, s, c, :], i_)
                    ins.then_inc(z("net_xe"), 1)

                def hidden(j, first):
                    v.wait_ge(z("net_mm1"), j + 1 + tiles_before)
                    if not first:
                        v.wait_ge(z("net_htr"), j + tiles_before)
                    v.tensor_copy(HS[:, 0:512], ps[1][:, 0:512])
                    v.tensor_copy(HS[:, 512:H], ps[2][:, 0:H - 512]).then_inc(z("net_hs"), 1)

                def result(j, s, e, h0, first):
                    v.wait_ge(z("net_mm2"), j + 1 + tiles_before)
                    if not first:
                        v.wait_ge(z(f"net_added{s}"), h0 + tiles_before * 8)
                    v.tensor_copy(SIDX[:, s:s + 1], sidx_t[:, bass.ds(j, 1)])
                    b_ = B2B[:, bass.ds(e * D, D)] if experts else FB2B
                    v.tensor_tensor(YO[:, s, :], ps[5 + s][:, 0:D], b_, ALU.add).then_inc(z("net_y"), 1)
                    v.wait_ge(z("net_y"), j + 1 + tiles_before)
                    v.tensor_scalar(YO[:, s, :], YO[:, s, :], gate_t[:, bass.ds(j, 1)], None, ALU.mult
                                    ).then_inc(z("net_out"), 1)

                stage_in(0, 0, 0, True)
                stage_in(1, 1, 0, True)
                normed(0, 0, e_(0))
                hidden(0, True)
                normed(1, 1, e_(1))
                stage_in(2, 0, 16, False)
                hidden(1, False)
                normed(2, 0, e_(2))
                stage_in(3, 1, 16, False)
                result(0, 0, e_(0), 0, True)
                def pair(j0, first):
                    h0 = j0 * 8
                    hidden(j0, False)
                    normed(j0 + 1, 1, e_(j0 + 1))
                    stage_in(j0 + 2, 0, h0 + 16, False)
                    result(j0 - 1, 1, e_(j0 - 1), None if first else h0 - 16, first)
                    hidden(j0 + 1, False)
                    normed(j0 + 2, 0, e_(j0 + 2))
                    stage_in(j0 + 3, 1, h0 + 16, False)
                    result(j0, 0, e_(j0), h0, False)
                pair(2, True)
                with v.Fori(4, tiles - 2, 2) as j0:
                    pair(j0, False)
                j0, h0 = tiles - 2, (tiles - 2) * 8
                hidden(j0, False)
                normed(j0 + 1, 1, e_(j0 + 1))
                result(j0 - 1, 1, e_(j0 - 1), h0 - 16, False)
                hidden(j0 + 1, False)
                result(j0, 0, e_(j0), h0, False)
                result(j0 + 1, 1, e_(j0 + 1), h0, False)

            def item_sums(tag):
                def onehot(i, j):
                    v.tensor_scalar(OH[:, j % 4, :], IOTA[:], DREL[:, bass.ds(i, 1)], None, ALU.is_equal
                                    ).then_inc(z(f"{tag}_oh"), 1)

                def body(i0):
                    for u in range(U):
                        i = i0 + u
                        if u % 4 == 0:
                            offs = load_offsets(DVE_, ROW_D, i, (T - 1) * (D + 1))
                        onehot(i + 2, u + 2)
                        v.wait_ge(z(f"{tag}_add"), i + 1)
                        v.wait_ge(z(f"{tag}_mm"), i + 1)
                        acc = ACCf[:, bass.ds(offs[u % 4], D + 1)]
                        v.tensor_tensor(acc, acc, ps[u % 4][:, 0:D + 1], ALU.add).then_inc(z(f"{tag}_add"), 1)
                step(v.memset(G[:, :, D:D + 1], 1.0))
                onehot(0, 0)
                onehot(1, 1)
                v.engine_nop().then_inc(z(f"{tag}_add"), 1)
                with v.Fori(0, NI - U, U) as i0:
                    body(i0)
                body(NI - U)

            v.wait_ge(z("s_add"), NIS + 1)
            step(v.tensor_scalar(DI, ACC[:, :, D], 1.0, None, ALU.max))
            inv_root("do", DO, DI)
            v.wait_ge(z("par_in"), PAR_IN)
            for c in range(NCH + 3):
                if c < NCH:
                    v.wait_ge(z("x1_set"), c + 1)
                    ln_stats("ln1", c, lambda i: X[:, c * CH + i, :])
                if 1 <= c <= NCH:
                    ln_scale("ln1", c - 1)
                if 2 <= c <= NCH + 1:
                    v.wait_ge(*norms("ln1", "norm", c - 1))
                    ln_stats("ln2", c - 2, lambda i: ACC[:, (c - 2) * CH + i, 0:D], 1)
                if c >= 3:
                    ln_scale("ln2", c - 3, 1)
            v.wait_ge(z("par_t"), 1)
            step(v.tensor_copy(PT[:], ps[3][:, 0:P]))
            for k in range(2):
                v.wait_ge(*rows_out(k, 0))
            v.wait_ge(z("tile_mm"), T)
            l3 = ps[2][:, 0:TE].rearrange("p (t e) -> p t e", e=NE)
            step(v.tensor_tensor(LG3, l3, per_column(BRB[:, 0:NE], T), ALU.add))
            step(v.tensor_reduce(RM, LG3, AX.X, ALU.max))
            step(v.tensor_tensor(LG3, LG3, per_node(RM), ALU.subtract))
            v.engine_nop().then_inc(z("logits_set"), 1)
            v.tensor_scalar(DESC, IOTA[:, 0:NE], -1.0, float(NE), ALU.mult, ALU.add)
            v.memset(VAL, 1.0)
            step(v.tensor_scalar(SC[:, 0:1], PCOL, float(N + 1), None, ALU.add))
            step(v.tensor_scalar(VAL[:, T - 1:T], PCOL, float(LAST), None, ALU.is_lt))
            v.wait_ge(z("exp_set"), 1)
            step(v.tensor_reduce(RM, PR3, AX.X, ALU.add))
            step(v.reciprocal(RM, RM))
            step(v.tensor_tensor(PR3, PR3, per_node(RM), ALU.mult))

            def largest(oh, m):
                step(v.tensor_reduce(m, PR3, AX.X, ALU.max))
                step(v.tensor_tensor(EQ3, PR3, per_node(m), ALU.is_equal))
                step(v.tensor_tensor(EQ3, EQ3, per_column(DESC, T), ALU.mult))
                step(v.tensor_reduce(RM, EQ3, AX.X, ALU.max))
                step(v.tensor_tensor(oh, EQ3, per_node(RM), ALU.is_equal))
            largest(OH1, GT[:, 0, :])
            step(v.scalar_tensor_tensor(PR, OHB[:, 0:TE], -2.0, PR, ALU.mult, ALU.add))
            largest(OH2, GT[:, 1, :])
            step(v.tensor_tensor(RM, GT[:, 0, :], GT[:, 1, :], ALU.add))
            step(v.reciprocal(RM, RM))
            for k, oh in enumerate((OH1, OH2)):
                step(v.tensor_tensor(GT[:, k, :], GT[:, k, :], RM, ALU.mult))
                step(v.tensor_tensor(oh, oh, per_node(VAL), ALU.mult))
            v.tensor_tensor(LG, OHB[:, 0:TE], OHB[:, TE:2 * TE], ALU.add).then_inc(z("choice_set"), 1)
            et = "p (e t) -> p e t"
            v.wait_ge(z("choice_rank"), 1)
            step(v.tensor_copy(EXC.rearrange(et, e=NE), ps[1][:, 0:TE].rearrange("p (t e) -> p e t", e=NE)))
            step(v.memset(EQ, 1.0))
            step(v.tensor_tensor_scan(INC[:, 0:TE], EQ, EXC, 0.0, ALU.mult, ALU.add))
            step(v.tensor_tensor(EXC, INC[:, 0:TE], EXC, ALU.subtract))
            end, start = INC[:, 0:TE].rearrange(et, e=NE)[:, :, T - 1], EXC.rearrange(et, e=NE)[:, :, 0]
            step(v.tensor_tensor(TLN, end, start, ALU.subtract))
            step(v.tensor_scalar(TLN, TLN, float(P - 1), None, ALU.add))
            step(v.tensor_copy(TLI, TLN))
            step(v.tensor_scalar(TLI, TLI, 7, None, ALU.arith_shift_right))
            step(v.tensor_copy(TLN, TLI))
            step(v.tensor_tensor_scan(TOFF, ONES[:, 0:NE], TLN, 0.0, ALU.mult, ALU.add))
            step(v.tensor_tensor(TOFF, TOFF, TLN, ALU.subtract))
            step(v.scalar_tensor_tensor(PB, TOFF, float(P), start, ALU.mult, ALU.subtract))
            r3 = ps[0][:, 0:TE].rearrange("p (t e) -> p t e", e=NE)
            step(v.tensor_tensor(PA, r3, EXC.rearrange("p (e t) -> p t e", e=NE), ALU.add))
            step(v.tensor_tensor(PA, PA, per_column(PB, T), ALU.add))
            for k, oh in enumerate((OH1, OH2)):
                step(v.tensor_tensor(oh, oh, PA, ALU.mult))
                step(v.tensor_reduce(PK[:, k, :], oh, AX.X, ALU.add))
            step(v.tensor_scalar(RM, VAL, -FAR, FAR, ALU.mult, ALU.add))
            for k in range(2):
                step(v.tensor_tensor(PK[:, k, :], PK[:, k, :], RM, ALU.add))
            step(v.tensor_scalar(IDT, IOTA[:, 0:T], float(P), PCOL, ALU.mult, ALU.add))
            step(v.tensor_scalar(IDT, IDT, 1.0, None, ALU.add))
            places(PK, 2)
            ef = work[:, 0:NT]
            step(v.tensor_scalar(ef, IOTA[:, 0:NT], TOFF[:, 1:2], None, ALU.is_ge))
            for e in range(2, NE):
                step(v.scalar_tensor_tensor(ef, IOTA[:, 0:NT], TOFF[:, e:e + 1], ef, ALU.is_ge, ALU.add))
            step(v.tensor_copy(etab[0:1, 0:NT], ef[0:1, :]))
            invert("moe", NT, 2 * T)
            network(**MOE)

            for c in range(NCH + 1):
                if c < NCH:
                    v.wait_ge(z(f"x_in{c}"), 16 * (2 + (c == NCH - 1)))
                    ln_stats("ln3", c, lambda i: X[:, c * CH + i, :])
                if c >= 1:
                    ln_scale("ln3", c - 1, extra=DO)
            v.wait_ge(z("acc1_zero"), 1)
            step(v.tensor_scalar(rows[0:1, ROW_D, :], rows[0:1, ROW_D, :], (D + 1) / D, None, ALU.mult))
            for k in range(2):
                v.wait_ge(*rows_out(k, 1))
            v.engine_nop().then_inc(z("conv_ready"), 1)
            item_sums("p1")
            v.wait_ge(z("p1_add"), NI + 1)
            step(v.tensor_scalar(RM, ACC[:, :, D], 1.0, None, ALU.max))
            inv_root("di", DI, RM)
            v.wait_ge(z("tail_in"), 8 * 16)

            def product(tag, l, t, to, bias):
                v.wait_ge(z("tile_mm"), t + 1 + TILES_BEFORE[tag])
                return v.scalar_tensor_tensor(to, ps[2 + t % 4][:, 0:D], DI[:, t:t + 1], bias, ALU.mult, ALU.add)
            for t in range(T):
                if t >= 2:
                    v.wait_ge(z("relu1"), t - 1)
                product("c1", 0, t, ZB[:, t % 2, :], GB1B).then_inc(z("lin1"), 1)
            v.memset(ACCf, 0.0).then_inc(z("acc2_zero"), 1)
            for k in range(2):
                v.wait_ge(*rows_out(k, 2))
            v.wait_ge(z("acc2_zero"), 1)
            v.engine_nop().then_inc(z("conv_ready"), 1)
            item_sums("p2")
            v.wait_ge(z("p2_add"), NI + 1)
            for t in range(T):
                product("c2", 1, t, ACC[:, t, 0:D], GB2B).then_inc(z("lin2"), 1)
                c = t // CH - 1
                if c >= 0 and t % CH == 0:
                    v.wait_ge(z("lin2"), (c + 1) * CH)
                    ln_stats("ln5", c, lambda i: ACC[:, c * CH + i, 0:D])
                if c >= 0 and t % CH == 4:
                    ln_scale("ln5", c)
            c = NCH - 1
            v.wait_ge(z("lin2"), T)
            ln_stats("ln5", c, lambda i: ACC[:, c * CH + i, 0:D])
            ln_scale("ln5", c)
            for c in range(NCH + 1):
                if c < NCH:
                    v.wait_ge(z("x3_set"), c + 1)
                    ln_stats("ln4", c, lambda i: X[:, c * CH + i, :], 1)
                if c >= 1:
                    ln_scale("ln4", c - 1, 1)
            for c in range(NCH):
                v.wait_ge(*norms("ln4", "norm", c + 1))
                for t in range(c * CH, (c + 1) * CH):
                    step(v.scalar_tensor_tensor(HS[:, 0:D], ACC[:, t, 0:D], 1.0, FWRB, ALU.mult, ALU.mult,
                                                accum_out=WV[:, t:t + 1]))
            step(v.tensor_scalar(WV, WV, FBR, None, ALU.add))

            ROUND = [0]

            def counted(ins, n=1):
                ins.then_inc(z("cnt_set"), 1)
                ROUND[0] += 1
                v.wait_ge(z("cnt_sum"), ROUND[0])
                return ps[1][:, 0:n]

            def count(scores, bound, op):
                return counted(v.scalar_tensor_tensor(T1, scores, bound, VAL, op, ALU.mult, accum_out=CNTS[:, 0:1]))
            THR, SIGN, KTH, NEED = (SC[:, k:k + 1] for k in range(2, 6))
            CAND, KEEP = SC[:, 6:13], SC[:, 13:20]
            total = count(WV, ZEROC, ALU.is_ge)
            step(v.tensor_scalar(SIGN, total, float(KSEL), None, ALU.is_ge))
            step(v.tensor_scalar(KTH, SIGN, float(2 * KSEL - N - 1), float(N - KSEL + 1), ALU.mult, ALU.add))
            step(v.tensor_scalar(SIGN, SIGN, 2.0, -1.0, ALU.mult, ALU.add))
            step(v.tensor_scalar(RM, WV, SIGN, None, ALU.mult))
            step(v.memset(THR, 0.0))
            for low, bits in SEARCH:
                n = (1 << bits) - 1
                for k in range(n):
                    ins = v.tensor_scalar(CAND[:, k:k + 1].bitcast(I32), THR.bitcast(I32), (k + 1) << low, None,
                                          ALU.bitwise_or)
                step(ins)
                for k in range(n):
                    ins = v.scalar_tensor_tensor(EQ[:, T * k:T * k + T], RM, CAND[:, k:k + 1], VAL, ALU.is_ge,
                                                 ALU.mult, accum_out=CNTS[:, k:k + 1])
                total = counted(ins, n)
                step(v.tensor_scalar(KEEP[:, 0:n], total, KTH, 3.0e38, ALU.is_ge, ALU.mult))
                step(v.tensor_tensor(KEEP[:, 0:n], CAND[:, 0:n], KEEP[:, 0:n], ALU.min))
                step(v.tensor_reduce(SC[:, 20:21], KEEP[:, 0:n], AX.X, ALU.max))
                step(v.tensor_tensor(THR, THR, SC[:, 20:21], ALU.max))
            step(v.tensor_scalar(THR, THR, SIGN, None, ALU.mult))
            total = count(WV, THR, ALU.is_gt)
            step(v.tensor_scalar(NEED, total, -1.0, float(KSEL), ALU.mult, ALU.add))
            step(v.scalar_tensor_tensor(EQ[:, 0:T], WV, THR, VAL, ALU.is_equal, ALU.mult))

            def prefix(n):
                v.engine_nop().then_inc(z("mark_set"), 1)
                v.wait_ge(z("mark_rank"), n)
                step(v.tensor_copy(EXC[:, 0:T], ps[1][:, 64:64 + T]))
                step(v.tensor_tensor_scan(INC[:, 0:T], ONES[:, 0:T], EXC[:, 0:T], 0.0, ALU.mult, ALU.add))
                step(v.tensor_tensor(EXC[:, 0:T], INC[:, 0:T], EXC[:, 0:T], ALU.subtract))
                step(v.tensor_tensor(EXC[:, 0:T], EXC[:, 0:T], ps[0][:, 0:T], ALU.add))
                return EXC[:, 0:T]
            r = prefix(1)
            step(v.scalar_tensor_tensor(RM, r, NEED, EQ[:, 0:T], ALU.is_lt, ALU.mult))
            step(v.scalar_tensor_tensor(T1, WV, THR, VAL, ALU.is_gt, ALU.mult))
            step(v.tensor_tensor(EQ[:, 0:T], RM, T1, ALU.add))
            r = prefix(2)
            step(v.tensor_scalar(IDT, IOTA[:, 0:T], float(P), PCOL, ALU.mult, ALU.add))
            step(v.scalar_tensor_tensor(RM, IDT, float(KSEL), r, ALU.add, ALU.subtract))
            step(v.tensor_tensor(T1, r, RM, ALU.subtract))
            step(v.tensor_tensor(T1, T1, EQ[:, 0:T], ALU.mult))
            step(v.tensor_tensor(T1, T1, RM, ALU.add))
            step(v.tensor_scalar(RM, VAL, -FAR, FAR, ALU.mult, ALU.add))
            step(v.tensor_tensor(PK[:, 0, :], T1, RM, ALU.add))
            step(v.tensor_tensor(WV, WV, EQ[:, 0:T], ALU.mult))
            step(v.tensor_scalar(IDT, IDT, 1.0, None, ALU.add))
            places(PK, 1)
            invert("ffn", NFT, T)
            v.wait_ge(z("sum_out"), 16 * (NCH + 1))
            network(**FFN)

        @block.tensor
        def _(pe):
            def totals(c, at, tag):
                if tag == "d":
                    pe.wait_ge(z("counted_d"), 1)
                else:
                    pe.wait_ge(z("counted_s"), 1)
                    pe.wait_ge(z("a_step"), T - B_ACT)
                pe.matmul(ps[0][:, at:at + 52], ONES[:], CNT[:, at:at + 52], start=True, stop=True
                          ).then_inc(z(f"totals_{tag}"), 1)
            row_no = [0]

            def rows_of():
                r = row_no[0]
                row_no[0] += 1
                pe.wait_ge(z("diag_set"), r + 1)
                if r:
                    pe.wait_ge(z("row_used"), 2 * r)
                d = DG.rearrange("p k n -> p (k n)")
                pe.matmul(ps[1][:, 0:512], ONES[:], d[:, 0:512], start=True, stop=True)
                pe.matmul(ps[2][:, 0:NIP - 512], ONES[:], d[:, 512:NIP], start=True, stop=True
                          ).then_inc(z("row_made"), 1)
            pe.wait_ge(z("const"), CONST)
            totals("d", 0, "d")
            pe.wait_ge(z("disorder_set"), 1)
            with pe.If(disorder(PE_) > 0):
                pe.matmul(ps[5][:, 0:T], ONES[0:1, :], ST[0:1, 0:T], start=True, stop=False, skip_group_check=True
                          ).then_inc(z("fix_rank"), 1)
                with pe.Fori(0, NBLK) as b_:
                    pe.wait_ge(z("fix_tile"), b_ + 1)
                    pe.matmul(ps[5][:, 0:T], TRIB[:, 0, :], BOH[:, 0, 0:T], start=False, stop=False,
                              skip_group_check=True).then_inc(z("fix_rank"), 1)
                    pe.wait_ge(z("fix_idx"), b_ + 1)
                    pe.matmul(ps[5][:, 0:T], TRIB[:, 1, :], BOH[:, 0, 0:T], start=False, stop=False,
                              skip_group_check=True).then_inc(z("fix_rank"), 1)
            rows_of()
            rows_of()
            totals("s", 52, "s")
            rows_of()
            rows_of()
            rows_of()
            for k in range(NIT):
                pe.wait_ge(z("rec_f"), k + 1)
                if k >= 2:
                    pe.wait_ge(z("rec_used"), k - 1)
                for a_ in range(3):
                    src_ = RF[:, k, a_, :] if a_ < 2 else recs[:, k, 2, :].bitcast(F32)
                    ins = pe.transpose(ps[3 + k % 2][:, a_ * P:(a_ + 1) * P], src_, IDENT[:])
                ins.then_inc(z("rec_t"), 1)

            def transpose_oh(i, j, wait_free):
                pe.wait_ge(z("m_oh"), i + 1)
                if wait_free:
                    pe.wait_ge(z("m_oht"), i - 1)
                pe.transpose(ps[j % 2][:, 0:P], OH[:, j % 4, :], IDENT[:]).then_inc(z("m_tr"), 1)
            pe.wait_ge(z("starts_set"), 1)
            pe.wait_ge(z("row_used"), 10)
            pe.matmul(ps[2][:, 0:T], ONES[0:1, :], STS[0:1, 0:T], start=True, stop=False, skip_group_check=True)
            pe.wait_ge(z("rec_used"), NIT)
            transpose_oh(0, 0, False)

            def rank(i, j, which, note):
                ins = pe.matmul(ps[2][:, 0:T], TRIB[:, which, :], BOH[:, j % 4, 0:T], start=False, stop=False,
                                skip_group_check=True)
                if note:
                    ins.then_inc(z("m_rank"), 1)
            pe.wait_ge(z("m_boh"), 1)
            rank(0, 0, 0, True)
            pe.wait_ge(*norms("ln0", "norm", NCH))

            def message_body(i0, first):
                for u in range(U):
                    i = i0 + u
                    if u % 4 == 0:
                        offs = load_offsets(PE_, ROW_D, i, (T - 1) * D)
                    transpose_oh(i + 1, u + 1, not (first and u < 1))
                    pe.wait_ge(z("m_pos"), i + 1)
                    rank(i, u, 1, False)
                    pe.wait_ge(z("m_boh"), i + 2)
                    rank(i + 1, u + 1, 0, True)
                    pe.wait_ge(z("m_oht"), i + 1)
                    if not (first and u < 2):
                        pe.wait_ge(z("m_row"), i - 1)
                    pe.matmul(ps[3 + u % 2][:, 0:D], OHT[:, u % 2, :], XNf[:, bass.ds(offs[u % 4], D)],
                              start=True, stop=True).then_inc(z("m_mm"), 1)
            pe.wait_ge(z("rows_set"), 5)
            message_body(0, True)
            with pe.Fori(U, NI, U) as i0:
                message_body(i0, False)

            def sum_body(i0, first):
                for u in range(U):
                    i = i0 + u
                    if u % 2 == 0:
                        pe.wait_ge(z("s_oh"), i + 2)
                        pe.wait_ge(z(f"sorted_in{u // 2}"), i0 + 16)
                    if u % 2 == 0 and not (first and u < 8):
                        pe.wait_ge(z("s_add"), i - 5)
                    pe.matmul(ps[u // 2 % 4][:, 0:D + 1], SOH[:, u % 8, :], G[:, u, 0:D + 1], start=(u % 2 == 0),
                              stop=(u % 2 == 1)).then_inc(z("s_mm"), 1)
            sum_body(0, True)
            with pe.Fori(U, NIS, U) as i0:
                sum_body(i0, False)

            def tile_products(tag, t, width, rhs, bank, at, between=None):
                def transposes(t_):
                    if t_ >= 2:
                        pe.wait_ge(z("tile_xt"), t_ - 1 + TILES_BEFORE[tag])
                    for c in range(KC):
                        ins = pe.transpose(ps[t_ % 2][:, c * P:(c + 1) * P], ACC[:, t_, c * P:(c + 1) * P], IDENT[:])
                    ins.then_inc(z("tile_tr"), 1)
                if t == 0:
                    transposes(0)
                if t + 1 < T:
                    if between is not None:
                        between(t + 1)
                    transposes(t + 1)
                pe.wait_ge(z("tile_xt"), t + 1 + TILES_BEFORE[tag])
                for c in range(KC):
                    ins = pe.matmul(ps[bank][:, at:at + width], XT[:, t % 2, c, :], rhs(c), start=(c == 0),
                                    stop=(c == KC - 1))
                ins.then_inc(z("tile_mm"), 1)

            def network(tag, tiles, tiles_before, **_):
                experts = tag == "moe"

                def e_(j):
                    return expert(PE_, j) if experts else None

                def transposes(j, s, h0, first):
                    pe.wait_ge(z(f"net_in{s}"), h0 + tiles_before * 8)
                    if not first:
                        pe.wait_ge(z("net_xe"), j + tiles_before)
                    for c in range(KC):
                        ins = pe.transpose(ps[0][:, c * P:(c + 1) * P], GX[:, s, c * P:(c + 1) * P], IDENT[:])
                    ins.then_inc(z("net_tr"), 1)

                def product1(j, s, e, first):
                    pe.wait_ge(z("net_xe"), j + 1 + tiles_before)
                    if not first:
                        pe.wait_ge(z("net_hs"), j + tiles_before)
                    for h in range(0, H, 512):
                        for c in range(KC):
                            w_ = (w1f[:, bass.ds(e * (KC * H) + (c * H + h), 512)] if experts
                                  else fw1s[:, c, h:h + 512])
                            ins = pe.matmul(ps[1 + h // 512][:, :], XE[:, s, c, :], w_, start=(c == 0),
                                            stop=(c == KC - 1))
                    ins.then_inc(z("net_mm1"), 1)

                def product2(j, s, e, first):
                    pe.wait_ge(z("net_gelu"), j + 1 + tiles_before)
                    if not first:
                        pe.wait_ge(z("net_y"), j - 1 + tiles_before)
                    for k in range(HC):
                        w_ = w2ff[:, bass.ds(e * (HC * D) + k * D, D)] if experts else fw2s[:, k, :]
                        ins = pe.matmul(ps[5 + s][:, 0:D], HTS[:, k, :], w_, start=(k == 0), stop=(k == HC - 1))
                    ins.then_inc(z("net_mm2"), 1)

                def hidden_t(j, first):
                    pe.wait_ge(z("net_hs"), j + 1 + tiles_before)
                    if not first:
                        pe.wait_ge(z("net_gelu"), j + tiles_before)
                    for k in range(HC):
                        ins = pe.transpose(ps[3 + k // 4][:, k % 4 * P:(k % 4 + 1) * P], HS[:, k * P:(k + 1) * P],
                                           IDENT[:])
                    ins.then_inc(z("net_htr"), 1)

                pe.wait_ge(z("slots"), 1 + (not experts))
                transposes(0, 0, 16, True)
                product1(0, 0, e_(0), True)
                transposes(1, 1, 16, False)
                hidden_t(0, True)
                product1(1, 1, e_(1), False)
                transposes(2, 0, 32, False)
                product2(0, 0, e_(0), True)
                hidden_t(1, False)
                def pair(j0, first):
                    h0 = j0 * 8
                    product1(j0, 0, e_(j0), False)
                    transposes(j0 + 1, 1, h0 + 16, False)
                    product2(j0 - 1, 1, e_(j0 - 1), first)
                    hidden_t(j0, False)
                    product1(j0 + 1, 1, e_(j0 + 1), False)
                    transposes(j0 + 2, 0, h0 + 32, False)
                    product2(j0, 0, e_(j0), False)
                    hidden_t(j0 + 1, False)
                pair(2, True)
                with pe.Fori(4, tiles - 2, 2) as j0:
                    pair(j0, False)
                j0, h0 = tiles - 2, (tiles - 2) * 8
                product1(j0, 0, e_(j0), False)
                transposes(j0 + 1, 1, h0 + 16, False)
                product2(j0 - 1, 1, e_(j0 - 1), False)
                hidden_t(j0, False)
                product1(j0 + 1, 1, e_(j0 + 1), False)
                product2(j0, 0, e_(j0), False)
                hidden_t(j0 + 1, False)
                product2(j0 + 1, 1, e_(j0 + 1), False)

            def inversion(tag, tiles, steps):
                pe.matmul(ps[2][:, 0:2 * tiles], ONES[0:1, :], ZERO[0:1, 0:2 * tiles], start=True, stop=False,
                          skip_group_check=True).then_inc(z(f"{tag}_inv"), 1)
                for n in range(steps):
                    pe.wait_ge(z(f"{tag}_scaled"), n + 1)
                    pe.matmul(ps[2][:, 0:2 * tiles], A_OH[:, n % 4, :], B_OH[:, n % 4, 0:2 * tiles], start=False,
                              stop=(n == steps - 1), skip_group_check=True).then_inc(z(f"{tag}_inv"), 1)

            def item_products(tag):
                def body(i0, first):
                    for u in range(U):
                        i = i0 + u
                        pe.wait_ge(z(f"{tag}_oh"), i + 1)
                        pe.wait_ge(z(f"ring_dma{u}"), i0 + (16 + BEFORE[tag]))
                        if not (first and u < 4):
                            pe.wait_ge(z(f"{tag}_add"), i - 2)
                        pe.matmul(ps[u % 4][:, 0:D + 1], OH[:, u % 4, :], G[:, u, 0:D + 1], start=True, stop=True
                                  ).then_inc(z(f"{tag}_mm"), 1)
                body(0, True)
                with pe.Fori(U, NI, U) as i0:
                    body(i0, False)

            pe.wait_ge(z("par_in"), PAR_IN)
            pe.wait_ge(z("s_add"), NIS + 1)
            pe.transpose(ps[3][:, 0:P], PT[:], IDENT[:]).then_inc(z("par_t"), 1)
            pe.wait_ge(*norms("ln1", "norm", 1))
            for t in range(T):
                def normed(t_):
                    pe.wait_ge(*norms("ln1", "norm", t_ // CH + 1))
                tile_products("rt", t, NE, lambda c: WRS[:, c, :], 2, t * NE, normed)
            pe.wait_ge(z("choice_set"), 1)
            pe.matmul(ps[0][:, 0:TE], TRI[:], LG, start=True, stop=True)
            pe.matmul(ps[1][:, 0:TE], ONES[:], LG, start=True, stop=True).then_inc(z("choice_rank"), 1)
            inversion("moe", NT, 2 * T)
            pe.wait_ge(z("w1_in"), 16 * NE)
            pe.wait_ge(z("w2_in"), 16 * NE)
            network(**MOE)
            pe.wait_ge(z("conv_ready"), 1)
            item_products("p1")
            pe.wait_ge(z("tail_in"), 8 * 16)
            pe.wait_ge(z("p1_add"), NI + 1)
            for t in range(T):
                if t >= 4:
                    pe.wait_ge(z("lin1"), t - 3)
                tile_products("c1", t, D, lambda c: gws[:, 0, c, :], 2 + t % 4, 0)
            pe.wait_ge(z("conv_ready"), 2)
            item_products("p2")
            pe.wait_ge(z("p2_add"), NI + 1)
            for t in range(T):
                if t >= 4:
                    pe.wait_ge(z("lin2"), t - 3)
                tile_products("c2", t, D, lambda c: gws[:, 1, c, :], 2 + t % 4, 0)
            for n, (_, bits) in enumerate([(0, 1)] + SEARCH + [(0, 1)]):
                pe.wait_ge(z("cnt_set"), n + 1)
                w_ = (1 << bits) - 1
                pe.matmul(ps[1][:, 0:w_], ONES[:], CNTS[:, 0:w_], start=True, stop=True).then_inc(z("cnt_sum"), 1)
            for n in range(2):
                pe.wait_ge(z("mark_set"), n + 1)
                pe.matmul(ps[0][:, 0:T], TRI[:], EQ[:, 0:T], start=True, stop=True)
                pe.matmul(ps[1][:, 64:64 + T], ONES[:], EQ[:, 0:T], start=True, stop=True).then_inc(z("mark_rank"), 1)
            inversion("ffn", NFT, T)
            pe.wait_ge(z("fw_in"), 32)
            network(**FFN)


_INS = ['x', 'src', 'dst', 'edge_weight', 'L0_ffn_Wr', 'L0_ffn_br', 'L0_ffn_ln_g', 'L0_ffn_ln_b', 'L0_ffn_W1',
        'L0_ffn_b1', 'L0_ffn_W2', 'L0_ffn_b2', 'L1_gnn_W1', 'L1_gnn_b1', 'L1_gnn_W2', 'L1_gnn_b2', 'L1_gnn_gamma',
        'L1_gnn_beta', 'L1_ffn_wr', 'L1_ffn_br', 'L1_ffn_w1', 'L1_ffn_b1', 'L1_ffn_w2', 'L1_ffn_b2']


def kernel(**inputs):
    import numpy as _np
    import concourse.bacc as _bacc
    from concourse import mybir as _mybir
    from concourse.bass_utils import run_bass_kernel_spmd as _run

    nc = _bacc.Bacc("TRN2", target_bir_lowering=False, num_devices=1)
    arrays, args = {}, []
    for name in _INS:
        a = _np.ascontiguousarray(inputs[name])
        arrays[f"in_{name}_dram"] = a
        args.append(nc.dram_tensor(f"in_{name}_dram", a.shape, _mybir.dt.from_np(a.dtype), kind="ExternalInput").ap())
    shape = inputs["x"].shape
    args.append(nc.dram_tensor("out_0_dram", shape, _mybir.dt.from_np(_np.dtype("float32")),
                               kind="ExternalOutput").ap())
    gnn_program(nc, *args)
    r = _run(nc, [arrays], core_ids=[0])
    return r.results[0]["out_0_dram"]
```
